# Optimizing a Trainium2 kernel written in Bass

```python
import numpy as np
import jax
import jax.numpy as jnp

def _softmax(x, axis=-1):
    return jax.nn.softmax(x, axis=axis)

def _gelu(x):
    return jax.nn.gelu(x, approximate=True)

def _silu(x):
    return jax.nn.silu(x)

def _sigmoid(x):
    return jax.nn.sigmoid(x)

def _layernorm(x, axis=-1, eps=1e-05):
    m = jnp.mean(x, axis=axis, keepdims=True)
    v = jnp.var(x, axis=axis, keepdims=True)
    return (x - m) / jnp.sqrt(v + eps)

def _scatter_add(tgt, idx, src, axis=0):
    return tgt.at[idx].add(src)

def _segment_sum(src, seg, n):
    return jax.ops.segment_sum(src, seg, n)
kernel_name = 'mk_gnn_preln_d1_gnn_r8_5e6148'

def setup_inputs(seed: int=0):
    np.random.seed(seed)
    _w = jnp.asarray

    def _rec_inputs():
        import jax
        import jax.numpy as jnp
        _gk = jax.random.key(seed)
        x = -0.0005121 + 1.001 * jax.random.normal(jax.random.fold_in(_gk, 1), (12500, 32), jnp.float32)
        src = jax.random.randint(jax.random.fold_in(_gk, 2), (400000,), 0, 12500, jnp.int32)
        dst = jax.random.randint(jax.random.fold_in(_gk, 3), (400000,), 0, 12500, jnp.int32)
        _o = jnp.argsort(dst, stable=True)
        src = src[_o]
        dst = dst[_o]
        edge_attr_16 = 0.00012405 + 0.99998 * jax.random.normal(jax.random.fold_in(_gk, 11), (400000, 16), jnp.float32)
        edge_type_8 = jax.random.randint(jax.random.fold_in(_gk, 13), (400000,), 0, 8, jnp.int32)
        node_type_4 = jax.random.randint(jax.random.fold_in(_gk, 14), (12500,), 0, 4, jnp.int32)
        return (x, src, dst, edge_attr_16, edge_type_8, node_type_4)
    x, src, dst, edge_attr_16, edge_type_8, node_type_4 = _rec_inputs()

    def _L0_gnn_setup():
        import jax, jax.numpy as jnp
        import numpy as np
        N = 12500
        E = 200000
        IN = 32
        OUT = 32
        NT = 4
        ET = 8
        ETE = 16
        ED = 16
        EAE = 16
        SLOPE = 0.2

        def _lrelu(v):
            return jnp.where(v >= 0, v, SLOPE * v)
        key = jax.random.key(seed)
        ks = jax.random.split(key, 10)
        x = jax.random.normal(ks[0], (N, IN), jnp.float32)
        edge_index = jax.random.randint(ks[1], (2, E), 0, N)
        node_type = jax.random.randint(ks[2], (N,), 0, NT)
        edge_type = jax.random.randint(ks[3], (E,), 0, ET)
        edge_attr = jax.random.normal(ks[4], (E, ED), jnp.float32)
        s = 1.0 / np.sqrt(IN)
        hetero_w = jax.random.uniform(ks[5], (NT, IN, OUT), jnp.float32, -s, s)
        hetero_b = jnp.zeros((NT, OUT), jnp.float32)
        edge_type_emb = jax.random.normal(ks[6], (ET, ETE), jnp.float32)
        edge_attr_w = jax.random.normal(ks[7], (ED, EAE), jnp.float32) / np.sqrt(ED)
        att_w = jax.random.normal(ks[8], (2 * OUT + ETE + EAE, 1), jnp.float32) * 0.1
        lin_w = jax.random.normal(ks[9], (OUT + EAE, OUT), jnp.float32) / np.sqrt(OUT + EAE)
        return dict(x=x, edge_attr=edge_attr, hetero_w=hetero_w, hetero_b=hetero_b, edge_type_emb=edge_type_emb, edge_attr_w=edge_attr_w, att_w=att_w, lin_w=lin_w, edge_index=edge_index, node_type=node_type, edge_type=edge_type)
    _L0_gnn_all = _L0_gnn_setup()
    _L0_gnn_in = {k: v for k, v in _L0_gnn_all.items() if k in ('hetero_w', 'hetero_b', 'edge_type_emb', 'edge_attr_w', 'att_w', 'lin_w')}
    del _L0_gnn_all
    return {'x': x, 'src': src, 'dst': dst, 'edge_attr_16': edge_attr_16, 'edge_type_8': edge_type_8, 'node_type_4': node_type_4, 'L0_gnn_hetero_w': _L0_gnn_in['hetero_w'], 'L0_gnn_hetero_b': _L0_gnn_in['hetero_b'], 'L0_gnn_edge_type_emb': _L0_gnn_in['edge_type_emb'], 'L0_gnn_edge_attr_w': _L0_gnn_in['edge_attr_w'], 'L0_gnn_att_w': _L0_gnn_in['att_w'], 'L0_gnn_lin_w': _L0_gnn_in['lin_w']}

def reference(x, src, dst, edge_attr_16, edge_type_8, node_type_4, L0_gnn_hetero_w, L0_gnn_hetero_b, L0_gnn_edge_type_emb, L0_gnn_edge_attr_w, L0_gnn_att_w, L0_gnn_lin_w):
    import jax
    import jax.numpy as jnp

    def _L0_gnn_ref(x, edge_attr, hetero_w, hetero_b, edge_type_emb, edge_attr_w, att_w, lin_w, edge_index, node_type, edge_type):
        import jax, jax.numpy as jnp
        import numpy as np
        N = 12500
        E = 200000
        IN = 32
        OUT = 32
        NT = 4
        ET = 8
        ETE = 16
        ED = 16
        EAE = 16
        SLOPE = 0.2

        def _lrelu(v):
            return jnp.where(v >= 0, v, SLOPE * v)
        xl = jnp.einsum('ni,nio->no', x, hetero_w[node_type]) + hetero_b[node_type]
        src, dst = (edge_index[0], edge_index[1])
        ete = _lrelu(edge_type_emb[edge_type])
        eae = _lrelu(edge_attr @ edge_attr_w)
        x_i = xl[dst]
        x_j = xl[src]
        alpha = _lrelu(jnp.concatenate([x_i, x_j, ete, eae], axis=-1) @ att_w)
        amax = jax.ops.segment_max(alpha, dst, num_segments=N)
        alpha = jnp.exp(alpha - amax[dst])
        denom = jax.ops.segment_sum(alpha, dst, num_segments=N)
        alpha = alpha / (denom[dst] + 1e-16)
        msg = jnp.concatenate([x_j, eae], axis=-1) @ lin_w * alpha
        out = jax.ops.segment_sum(msg, dst, num_segments=N)
        return out
    edge_index = jnp.stack([src, dst])
    h = jnp.maximum(_layernorm(x, axis=-1), 0.0)
    x = x + _L0_gnn_ref(h, edge_attr_16, L0_gnn_hetero_w, L0_gnn_hetero_b, L0_gnn_edge_type_emb, L0_gnn_edge_attr_w, L0_gnn_att_w, L0_gnn_lin_w, edge_index, node_type_4, edge_type_8)
    return x

_drawn_inputs = setup_inputs


def setup_inputs(seed=0):
    import zlib

    import numpy as np

    out = dict(_drawn_inputs(seed))
    spreads = {'L0_gnn_hetero_b': (0.0, 0.1)}
    factors = {'L0_gnn_edge_type_emb': 4.747}
    for name, (base, spread) in spreads.items():
        noise = np.random.default_rng([zlib.crc32(name.encode()), seed]).standard_normal(out[name].shape)
        drawn = base * np.exp(spread * noise) if base else spread * noise
        out[name] = jnp.asarray(drawn.astype(out[name].dtype))
    for name, factor in factors.items():
        out[name] = (out[name] * factor).astype(out[name].dtype)
    return out
```

```python
import concourse.bass as bass
from concourse import mybir
from contextlib import ExitStack

N_NODES = 12500
N_EDGES = 400000
F_IN = 32
F_EDGE = 16
N_NODE_TYPES = 4
N_EDGE_TYPES = 8
SLOPE = 0.2

P = 128
EPP = N_EDGES // P
NPP = -(-N_NODES // P)
N_PAD = P * NPP
T = 25
CHUNKS = EPP // T
U = 5
ITERS = CHUNKS // U
G = 5
TG = T // G
YW = F_IN + 2
VW = F_IN + 1
RW = F_IN + 3
META = 3 * T + 1
BIG = 3.0e38
ROUND = 12582912.0
N7 = 7
NODE_ITERS = NPP // N7
BLK = 625
NBLK = N_EDGES // BLK


def gnn_kernel(nc, x, meta, dst_rows, dst_tmajor, dst_last_of_block, row_edges, row_last, edge_attr_t, node_type,
               hetero_wT, hetero_bT, edge_type_emb, edge_attr_w, att_w, lin_w, out):
    fp32, bf16, i32 = mybir.dt.float32, mybir.dt.bfloat16, mybir.dt.int32
    ALU, ACT, AX = mybir.AluOpType, mybir.ActivationFunctionType, mybir.AxisListType
    ds = bass.ds

    table_dram = nc.dram_tensor("table_dram", (N_PAD, YW), fp32, kind="Internal").ap()
    dst_hi_dram = nc.dram_tensor("dst_hi_dram", (CHUNKS, T * P), bf16, kind="Internal").ap()
    dst_f_dram = nc.dram_tensor("dst_f_dram", (NBLK, BLK), fp32, kind="Internal").ap()
    rows_dram = nc.dram_tensor("rows_dram", (N_EDGES, RW), fp32, kind="Internal").ap()
    rows_pm = rows_dram.rearrange("(p e) f -> p e f", p=P)

    ctx = ExitStack()
    with ctx:
        def sb(name, shape, dt=fp32):
            return ctx.enter_context(nc.sbuf_tensor(name, shape, dt))

        def sem(name):
            return ctx.enter_context(nc.semaphore(name))

        ident = sb("ident", [P, P])
        part = sb("part", [P, 1])
        free98 = sb("free98", [P, NPP])
        free128 = sb("free128", [P, P])
        node_id = sb("node_id", [P, NPP])
        types8 = sb("types8", [P, N_EDGE_TYPES])
        scores_w = sb("scores_w", [F_IN, YW])
        het_wT = sb("het_wT", [F_IN, P])
        het_bT = sb("het_bT", [F_IN, N_NODE_TYPES])
        node_w = sb("node_w", [P, YW])
        node_b = sb("node_b", [N_NODE_TYPES, YW])
        attr_w = sb("attr_w", [G * F_EDGE, G * F_EDGE])
        msg_w = sb("msg_w", [G * F_EDGE, G * VW])
        emb = sb("emb", [P, N_EDGE_TYPES, F_EDGE])
        emb_act = sb("emb_act", [P, N_EDGE_TYPES, F_EDGE])
        att_type = sb("att_type", [P, F_EDGE])
        type_score = sb("type_score", [P, N_EDGE_TYPES])

        x_sb = sb("x_sb", [P, NPP, F_IN])
        h = sb("h", [P, NPP, F_IN])
        node_buf = sb("node_buf", [P, NPP * RW])
        table = node_buf[:, 0:NPP * YW].rearrange("p (n f) -> p n f", f=YW)
        last_rows = node_buf[:].rearrange("p (n f) -> p n f", f=RW)
        stat = sb("stat", [P, 4, NPP])
        ntype = sb("ntype", [P, NPP], i32)
        ntype_f = sb("ntype_f", [P, NPP])
        tmask = sb("tmask", [P, NPP, N_NODE_TYPES])
        hm = sb("hm", [P, N7, P + N_NODE_TYPES])
        hmT = sb("hmT", [P, N7, P])
        maskT = sb("maskT", [N_NODE_TYPES, N7, P])
        s_rest = sb("s_rest", [P, NPP])
        s_dst = sb("s_dst", [P, 3, NPP], bf16)

        dst_f = sb("dst_f", [P, EPP])
        hi_f = sb("hi_f", [P, EPP])
        dst_i = hi_f[:].bitcast(i32)
        meta_sb = [sb(f"meta{u}", [P, META], i32) for u in range(U)]
        attr_sb = [sb(f"attr{u}", [G * F_EDGE, TG * P]) for u in range(U)]
        hib_sb = [sb(f"hib{u}", [P, T * P], bf16) for u in range(U)]
        gath = [sb(f"gath{u}", [P, T, YW]) for u in range(U)]
        rows = [sb(f"rows{u}", [P, T, RW]) for u in range(U)]
        onehot = sb("onehot", [P, T * P], bf16)
        hi_b = onehot[:, 0:EPP]
        eae_s = sb("eae_s", [G * F_EDGE, 2, TG * P // 2])
        eae = sb("eae", [G * F_EDGE, 2, TG * P // 2])
        dstc = sb("dstc", [P, T + 1])
        hic = sb("hic", [P, T])
        loc = sb("loc", [P, T])
        pen = sb("pen", [P, T])
        etc = sb("etc", [P, T])
        emask = sb("emask", [P, T, N_EDGE_TYPES])
        escore = sb("escore", [P, T])
        pick = h[:].rearrange("p n f -> p (n f)")[:, 0:T * NPP].rearrange("p (t n) -> p t n", n=NPP)
        dscore = sb("dscore", [P, T])
        msg = sb("msg", [P, T, VW])
        alpha = sb("alpha", [P, T])
        mrun = sb("mrun", [P, T + 1])
        args = sb("args", [P, 2, T])
        wts = sb("wts", [P, 2, T])
        terms = sb("terms", [P, VW, T + 1])
        keep = sb("keep", [P, VW, T + 1])
        sums = sb("sums", [P, VW, T + 1])

        blk_last_i = sb("blk_last_i", [P, NBLK], i32)
        blk_last = sb("blk_last", [P, NBLK])
        cnt_tmp = sb("cnt_tmp", [P, NBLK])
        nblk = sb("nblk", [P, NPP])
        incnt = sb("incnt", [P, NPP])
        blk_idx = [sb(f"blk_idx{j}", [P, 1], i32) for j in range(N7)]
        blk = [b[:].rearrange("p a b -> p (a b)")[:, 0:BLK] for b in gath + [msg, terms]]
        pos = sb("pos", [P, NPP], i32)
        redge_i = sb("redge_i", [P, 4], i32)
        redge = sb("redge", [P, 4])
        rlast_i = sb("rlast_i", [P, P], i32)
        rlast = sb("rlast", [P, P])
        head = sb("head", [P, 8])
        head_idx = sb("head_idx", [P, 2], i32)
        own = sb("own", [P, RW])
        tails = sb("tails", [P, RW])
        contrib = sb("contrib", [P, P])
        mtail = sb("mtail", [P, P])
        wtail = sb("wtail", [P, P])
        wtailT = sb("wtailT", [P, P])
        fix = sb("fix", [P, 4])
        joined = sb("joined", [P, RW])
        scale = sb("scale", [P, 2, NPP])

        def bank(name, n=1):
            return ctx.enter_context(nc.psum_tensor(name, [P, n, 512], fp32))

        ps_attr = bank("ps_attr", 2)
        ps_msg = bank("ps_msg", 2)
        ps_pick = bank("ps_pick", 2)
        ps_misc = bank("ps_misc")

        weights_in = sem("weights_in")
        zeroed = sem("zeroed")
        diag_in = sem("diag_in")
        x_in = sem("x_in")
        dst_in = sem("dst_in")
        consts = sem("consts")
        dve_step = sem("dve_step")
        act_step = sem("act_step")
        node_w_mm = sem("node_w_mm")
        node_w_sb = sem("node_w_sb")
        var_ready = sem("var_ready")
        dev_ready = sem("dev_ready")
        hm_ready = sem("hm_ready")
        hmT_mm = sem("hmT_mm")
        hmT_sb = sem("hmT_sb")
        tab_mm = sem("tab_mm")
        tab_sb = sem("tab_sb")
        table_out = sem("table_out")
        hi_ready = sem("hi_ready")
        hi_out = sem("hi_out")
        s_parts = sem("s_parts")
        gather_turns = sem("gather_turns")
        meta_in = [sem(f"meta_in{u}") for u in range(U)]
        attr_in = [sem(f"attr_in{u}") for u in range(U)]
        hib_in = [sem(f"hib_in{u}") for u in range(U)]
        gathered = [sem(f"gathered{u}") for u in range(U)]
        stored = [sem(f"stored{u}") for u in range(U)]
        attr_mm = sem("attr_mm")
        eae_scaled = sem("eae_scaled")
        eae_ready = sem("eae_ready")
        msg_mm = sem("msg_mm")
        msg_added = sem("msg_added")
        onehot_ready = sem("onehot_ready")
        pick_mm = sem("pick_mm")
        picked = sem("picked")
        args_ready = sem("args_ready")
        exp_done = sem("exp_done")
        keep_ready = sem("keep_ready")
        sums_ready = sem("sums_ready")
        rows_sums = sem("rows_sums")
        blk_idx_ready = sem("blk_idx_ready")
        blk_in = [sem(f"blk_in{j}") for j in range(N7)]
        blk_counted = sem("blk_counted")
        head_idx_ready = sem("head_idx_ready")
        own_in = sem("own_in")
        tails_in = sem("tails_in")
        mtail_mm = sem("mtail_mm")
        targs_ready = sem("targs_ready")
        texp_done = sem("texp_done")
        wtailT_mm = sem("wtailT_mm")
        wtailT_sb = sem("wtailT_sb")
        tsum_mm = sem("tsum_mm")
        joined_ready = sem("joined_ready")
        joined_out = sem("joined_out")
        last_in = sem("last_in")
        out_ready = sem("out_ready")
        out_done = sem("out_done")

        def count(n):
            return n + 1

        def start_at_one(eng, *sems):
            for s in sems:
                eng.sem_inc(s, 1)

        block = ctx.enter_context(nc.Block())

        @block.sync
        def _(sp):
            sp.dma_start(x_sb[:], x).then_inc(x_in, 16)
            sp.dma_start(ntype[:], node_type).then_inc(x_in, 16)
            for dst, src in ((scores_w[:, 0:F_IN], lin_w[0:F_IN, :]),
                             (scores_w[:, F_IN:F_IN + 1], att_w[F_IN:2 * F_IN, :]),
                             (scores_w[:, F_IN + 1:F_IN + 2], att_w[0:F_IN, :]),
                             (het_wT[:], hetero_wT), (het_bT[:], hetero_bT),
                             (emb[:], edge_type_emb.partition_broadcast(P)),
                             (att_type[:], att_w[2 * F_IN:2 * F_IN + F_EDGE, 0].partition_broadcast(P)),
                             (blk_last_i[:], dst_last_of_block.partition_broadcast(P)),
                             (redge_i[:], row_edges), (rlast_i[:], row_last.partition_broadcast(P))):
                sp.dma_start(dst, src).then_inc(weights_in, 16)
            sp.dma_start(dst_i, dst_tmajor).then_inc(dst_in, 16)
            sp.wait_ge(zeroed, 2)
            for g in range(G):
                k = slice(g * F_EDGE, (g + 1) * F_EDGE)
                sp.dma_start(attr_w[k, k], edge_attr_w).then_inc(diag_in, 16)
                sp.dma_start(msg_w[k, g * VW:g * VW + F_IN], lin_w[F_IN:F_IN + F_EDGE, :]).then_inc(diag_in, 16)
                sp.dma_start(msg_w[k, g * VW + F_IN:(g + 1) * VW],
                             att_w[2 * F_IN + F_EDGE:2 * F_IN + 2 * F_EDGE, :]).then_inc(diag_in, 16)
            sp.wait_ge(hi_ready, 1)
            sp.dma_start(dst_hi_dram.rearrange("c (a b) -> (c a b)", a=1).rearrange("(p e) -> p e", p=P),
                         hi_b).then_inc(hi_out, 16)
            sp.dma_start(dst_i, dst_rows).then_inc(dst_in, 16)
            sp.wait_ge(hi_ready, 2)
            sp.dma_start(dst_f_dram.rearrange("a b -> (a b)").rearrange("(p e) -> p e", p=P),
                         dst_f[:]).then_inc(hi_out, 16)
            sp.wait_ge(tab_sb, count(NODE_ITERS))
            sp.dma_start(table_dram.rearrange("(p n) f -> p n f", p=P), table).then_inc(table_out, 16)
            sp.wait_ge(hi_out, 32)

            def load_chunk(c, u):
                sp.dma_start(meta_sb[u][:], meta[:, ds(c, 1), :].rearrange("p a m -> p (a m)")).then_inc(
                    meta_in[u], 16)
                sp.dma_start(hib_sb[u][:], dst_hi_dram[ds(c, 1), :].rearrange("a e -> (a e)")
                             .partition_broadcast(P)).then_inc(hib_in[u], 16)
                sp.dma_start(attr_sb[u][:], edge_attr_t[:, ds(c, 1), :].rearrange("k a m -> k (a m)")).then_inc(
                    attr_in[u], 16)

            for u in range(U):
                load_chunk(u, u)
            with sp.Fori(1, ITERS) as i:
                for u in range(U):
                    sp.wait_ge(sums_ready, count(i * U + u + 1 - U))
                    load_chunk(i * U + u, u)
            for u in range(U):
                sp.wait_ge(stored[u], 16 * ITERS)
            sp.dma_start(tails[:], rows_pm[:, EPP - 1, :]).then_inc(tails_in, 16)
            sp.wait_ge(out_ready, 1)
            sp.dma_start(out, h[:]).then_inc(out_done, 16)
            sp.wait_ge(out_done, 16)
            sp.wait_ge(table_out, 16)

        @block.gpsimd
        def _(pool):
            nc.gpsimd.memset(attr_w[:], 0.0).then_inc(zeroed, 1)
            nc.gpsimd.memset(msg_w[:], 0.0).then_inc(zeroed, 1)
            nc.gpsimd.memset(ident[:], 0.0).then_inc(consts, 1)
            pool.wait_ge(consts, 1)
            nc.gpsimd.affine_select(out=ident[:], in_=ident[:], compare_op=ALU.not_equal, fill=1.0, base=0,
                                    pattern=[[-1, P]], channel_multiplier=1).then_inc(consts, 1)
            for tile, base, step, mult in ((part, 0, 0, 1), (free98, 0, 1, 0), (free128, 0, 1, 0),
                                           (node_id, 0, 1, NPP), (types8, 0, 1, 0)):
                nc.gpsimd.iota(tile[:], [[step, tile.shape[1]]], base=base, channel_multiplier=mult,
                               allow_small_or_imprecise_dtypes=True).then_inc(consts, 1)
            pool.wait_ge(table_out, 16)
            with pool.Fori(0, ITERS) as i:
                for u in range(U):
                    pool.wait_ge(meta_in[u], (i + 1) * 16)
                    pool.sem_inc(gather_turns, 1)
                    for t in range(T):
                        nc.gpsimd.indirect_dma_start(
                            gath[u][:, t, :], None, table_dram,
                            bass.IndirectOffsetOnAxis(ap=meta_sb[u][:, t:t + 1], axis=0)).then_inc(gathered[u], 16)
            pool.wait_ge(hi_out, 32)
            with pool.Fori(0, NODE_ITERS) as i:
                for j in range(N7):
                    pool.wait_ge(blk_idx_ready, i * N7 + j + 1)
                    pool.sem_inc(gather_turns, 1)
                    nc.gpsimd.indirect_dma_start(
                        blk[j], None, dst_f_dram,
                        bass.IndirectOffsetOnAxis(ap=blk_idx[j][:], axis=0)).then_inc(blk_in[j], 16)
            pool.wait_ge(head_idx_ready, 1)
            for u in range(U):
                pool.wait_ge(stored[u], 16 * ITERS)
            nc.gpsimd.indirect_dma_start(own[:], None, rows_dram,
                                         bass.IndirectOffsetOnAxis(ap=head_idx[:, 0:1], axis=0)).then_inc(own_in, 16)
            pool.wait_ge(joined_ready, 1)
            nc.gpsimd.indirect_dma_start(rows_dram, bass.IndirectOffsetOnAxis(ap=head_idx[:, 1:2], axis=0),
                                         joined[:], None, bounds_check=N_EDGES - 1, oob_is_err=False).then_inc(
                joined_out, 16)
            pool.wait_ge(joined_out, 16)
            for n in range(NPP):
                nc.gpsimd.indirect_dma_start(
                    last_rows[:, n, :], None, rows_dram,
                    bass.IndirectOffsetOnAxis(ap=pos[:, n:n + 1], axis=0)).then_inc(last_in, 16)

        @block.scalar
        def _(act):
            start_at_one(act, hmT_sb, rows_sums)
            act.wait_ge(node_w_mm, 1)
            nc.scalar.copy(node_w[:], ps_misc[:, 0, 0:YW])
            nc.scalar.copy(node_b[:], ps_misc[0:N_NODE_TYPES, 0, YW:2 * YW]).then_inc(node_w_sb, 1)
            act.wait_ge(var_ready, 1)
            nc.scalar.sqrt(stat[:, 3, :], stat[:, 2, :]).then_inc(dev_ready, 1)
            with act.Fori(0, NODE_ITERS) as i:
                act.wait_ge(hmT_mm, count(i + 1))
                act.wait_ge(tab_mm, count(i))
                nc.scalar.copy(hmT[:, 0:4, :], ps_attr[:, 0, :].rearrange("p (a b) -> p a b", b=P))
                nc.scalar.copy(hmT[:, 4:N7, :], ps_attr[:, 1, 0:3 * P].rearrange("p (a b) -> p a b", b=P))
                nc.scalar.copy(maskT[:, 0:4, :], ps_msg[0:N_NODE_TYPES, 0, :].rearrange("p (a b) -> p a b", b=P))
                nc.scalar.copy(maskT[:, 4:N7, :], ps_msg[0:N_NODE_TYPES, 1, 0:3 * P].rearrange(
                    "p (a b) -> p a b", b=P)).then_inc(hmT_sb, 1)
            with act.Fori(0, ITERS) as i:
                for u in range(U):
                    c = i * U + u
                    act.wait_ge(attr_mm, c + 1)
                    act.wait_ge(eae_ready, count(c))
                    nc.scalar.mul(eae_s[:], ps_attr[0:G * F_EDGE, :, 0:TG * P // 2], SLOPE).then_inc(eae_scaled, 1)
                    act.wait_ge(args_ready, c + 1)
                    nc.scalar.activation(wts[:], args[:], ACT.Exp).then_inc(exp_done, 1)
                    nc.scalar.copy(rows[u][:, :, VW], mrun[:, 1:T + 1])
                    nc.scalar.copy(rows[u][:, :, VW + 1], dstc[:, 1:T + 1])
                    act.wait_ge(exp_done, c + 1)
                    act.wait_ge(sums_ready, count(c))
                    nc.scalar.copy(keep[:, :, 1:T + 1], wts[:, 1:2, :].broadcast_to([P, VW, T])).then_inc(
                        keep_ready, 1)
                    act.wait_ge(sums_ready, count(c + 1))
                    nc.scalar.copy(rows[u][:, :, 0:VW], sums[:, :, 1:T + 1].rearrange("p f t -> p t f")).then_inc(
                        rows_sums, 1)
                    act.wait_ge(rows_sums, count(c + 1))
                    act.dma_start(rows_pm[:, ds(c * T, T), :], rows[u][:]).then_inc(stored[u], 16)
                for u in range(U):
                    act.wait_ge(stored[u], (i + 1) * 16)
            act.wait_ge(targs_ready, 1)
            nc.scalar.activation(wtail[:], mtail[:], ACT.Exp)
            nc.scalar.activation(fix[:, 2:3], fix[:, 1:2], ACT.Exp).then_inc(texp_done, 1)

        @block.tensor
        def _(pe):
            start_at_one(pe, hmT_mm, tab_mm, pick_mm, msg_mm)
            pe.wait_ge(weights_in, 10 * 16)
            nc.tensor.matmul(ps_misc[:, 0, 0:YW], het_wT[:], scores_w[:], start=True, stop=True)
            nc.tensor.matmul(ps_misc[0:N_NODE_TYPES, 0, YW:2 * YW], het_bT[:], scores_w[:], start=True,
                             stop=True).then_inc(node_w_mm, 1)
            pe.wait_ge(consts, 2)
            pe.wait_ge(node_w_sb, 1)
            with pe.Fori(0, NODE_ITERS) as i:
                pe.wait_ge(hm_ready, i + 1)
                pe.wait_ge(hmT_sb, count(i))
                for j in range(N7):
                    nc.tensor.transpose(ps_attr[:, j // 4, j % 4 * P:(j % 4 + 1) * P], hm[:, j, 0:P], ident[:])
                for j in range(N7):
                    last = nc.tensor.transpose(ps_msg[0:N_NODE_TYPES, j // 4, j % 4 * P:(j % 4 + 1) * P],
                                               hm[:, j, P:P + N_NODE_TYPES], ident[:])
                last.then_inc(hmT_mm, 1)
                pe.wait_ge(hmT_sb, count(i + 1))
                pe.wait_ge(tab_sb, count(i))
                for j in range(N7):
                    to = ps_misc[:, 0, j * YW:(j + 1) * YW]
                    nc.tensor.matmul(to, hmT[:, j, :], node_w[:], start=True, stop=False)
                    last = nc.tensor.matmul(to, maskT[:, j, :], node_b[:], start=False, stop=True)
                last.then_inc(tab_mm, 1)
            pe.wait_ge(s_parts, 1)
            pe.wait_ge(diag_in, 3 * G * 16)
            with pe.Fori(0, ITERS) as i:
                for u in range(U):
                    c = i * U + u
                    pe.wait_ge(attr_in[u], (i + 1) * 16)
                    pe.wait_ge(eae_ready, count(c))
                    for b in range(2):
                        last = nc.tensor.matmul(ps_attr[0:G * F_EDGE, b, 0:TG * P // 2], attr_w[:],
                                                attr_sb[u][:, b * (TG * P // 2):(b + 1) * (TG * P // 2)],
                                                start=True, stop=True)
                    last.then_inc(attr_mm, 1)
                    pe.wait_ge(onehot_ready, c + 1)
                    for g in range(TG):
                        pe.wait_ge(picked, count((c * TG + (g - 1 if g else 0)) * G))
                        for j in range(G):
                            t = g * G + j
                            for k in range(3):
                                last = nc.tensor.matmul(ps_pick[:, g % 2, j * NPP:(j + 1) * NPP],
                                                        onehot[:, t * P:(t + 1) * P], s_dst[:, k, :],
                                                        start=(k == 0), stop=(k == 2))
                        last.then_inc(pick_mm, 1)
                    pe.wait_ge(eae_ready, count(c + 1))
                    pe.wait_ge(msg_added, count(c))
                    eae_flat = eae[:].rearrange("k a b -> k (a b)")
                    for g in range(TG):
                        last = nc.tensor.matmul(ps_msg[:, g // 3, g % 3 * G * VW:(g % 3 + 1) * G * VW],
                                                eae_flat[:, g * P:(g + 1) * P], msg_w[:], start=True, stop=True)
                    last.then_inc(msg_mm, 1)
            pe.wait_ge(tails_in, 16)
            pe.wait_ge(head_idx_ready, 1)
            nc.tensor.transpose(ps_misc[:, 0, 0:P], mtail[:], ident[:]).then_inc(mtail_mm, 1)
            pe.wait_ge(texp_done, 1)
            nc.tensor.transpose(ps_misc[:, 0, P:2 * P], wtail[:], ident[:]).then_inc(wtailT_mm, 1)
            pe.wait_ge(wtailT_sb, 1)
            nc.tensor.matmul(ps_misc[:, 0, 2 * P:2 * P + VW], wtailT[:], tails[:, 0:VW], start=True,
                             stop=True).then_inc(tsum_mm, 1)

        @block.vector
        def _(dve):
            v = nc.vector
            start_at_one(dve, tab_sb, eae_ready, picked, msg_added, sums_ready)
            steps = [0]

            def done(ins, at=0):
                steps[0] += 1
                ins.then_inc(dve_step, 1)
                dve.wait_ge(dve_step, at + steps[0])

            v.memset(keep[:, :, 0:1], 0.0)
            v.memset(sums[:], 0.0)
            done(v.memset(mrun[:], 0.0))
            dve.wait_ge(x_in, 32)
            sq = table[:, :, 0:F_IN]
            done(v.tensor_reduce(stat[:, 0, :], x_sb[:], AX.X, ALU.add))
            done(v.tensor_scalar(stat[:, 1, :], stat[:, 0, :], 1.0 / F_IN, None, ALU.mult))
            done(v.tensor_tensor(h[:], x_sb[:], stat[:, 1, :].unsqueeze(2).broadcast_to([P, NPP, F_IN]), ALU.subtract))
            done(v.tensor_tensor(sq, h[:], h[:], ALU.mult))
            done(v.tensor_reduce(stat[:, 0, :], sq, AX.X, ALU.add))
            v.tensor_scalar(stat[:, 2, :], stat[:, 0, :], 1.0 / F_IN, 1e-5, ALU.mult, ALU.add).then_inc(var_ready, 1)
            done(v.tensor_copy(ntype_f[:], ntype[:]))
            dve.wait_ge(consts, 7)
            done(v.tensor_tensor(tmask[:], ntype_f[:].unsqueeze(2).broadcast_to([P, NPP, N_NODE_TYPES]),
                                 types8[:, 0:N_NODE_TYPES].unsqueeze(1).broadcast_to([P, NPP, N_NODE_TYPES]),
                                 ALU.is_equal))
            dve.wait_ge(dev_ready, 1)
            done(v.reciprocal(stat[:, 0, :], stat[:, 3, :]))
            done(v.scalar_tensor_tensor(h[:], h[:], 0.0, stat[:, 0, :].unsqueeze(2).broadcast_to([P, NPP, F_IN]),
                                        ALU.max, ALU.mult))
            with dve.Fori(0, NODE_ITERS) as i:
                dve.wait_ge(hmT_mm, count(i))
                v.tensor_tensor(hm[:, :, 0:P].rearrange("p n (k f) -> p n k f", f=F_IN),
                                h[:, ds(i * N7, N7), :].unsqueeze(2).broadcast_to([P, N7, N_NODE_TYPES, F_IN]),
                                tmask[:, ds(i * N7, N7), :].unsqueeze(3).broadcast_to([P, N7, N_NODE_TYPES, F_IN]),
                                ALU.mult)
                v.tensor_copy(hm[:, :, P:P + N_NODE_TYPES], tmask[:, ds(i * N7, N7), :]).then_inc(hm_ready, 1)
                dve.wait_ge(tab_mm, count(i + 1))
                v.tensor_scalar(table[:, ds(i * N7, N7), :],
                                ps_misc[:, 0, 0:N7 * YW].rearrange("p (n f) -> p n f", f=YW), 1.0, None,
                                ALU.mult).then_inc(tab_sb, 1)
            dve.wait_ge(tab_sb, count(NODE_ITERS))
            score = table[:, :, F_IN + 1]
            done(v.tensor_copy(s_dst[:, 0, :], score))
            done(v.tensor_tensor(s_rest[:], score, s_dst[:, 0, :], ALU.subtract))
            done(v.tensor_copy(s_dst[:, 1, :], s_rest[:]))
            done(v.tensor_tensor(s_rest[:], s_rest[:], s_dst[:, 1, :], ALU.subtract))
            v.tensor_copy(s_dst[:, 2, :], s_rest[:]).then_inc(s_parts, 1)

            def div98(to, src, at=0):
                done(v.tensor_scalar(to, src, 1.0 / NPP, 0.5 / NPP - 0.5, ALU.mult, ALU.add), at)
                done(v.tensor_scalar(to, to, ROUND, ROUND, ALU.add, ALU.subtract), at)

            dve.wait_ge(dst_in, 16)
            done(v.tensor_copy(dst_f[:], dst_i))
            div98(hi_f[:], dst_f[:])
            v.tensor_copy(hi_b, hi_f[:]).then_inc(hi_ready, 1)
            dve.wait_ge(dst_in, 32)
            v.tensor_copy(dst_f[:], dst_i).then_inc(hi_ready, 1)
            dve.wait_ge(weights_in, 10 * 16)
            done(v.scalar_tensor_tensor(emb_act[:], emb[:], SLOPE, emb[:], ALU.mult, ALU.max))
            done(v.tensor_tensor(emb_act[:], emb_act[:], att_type[:].unsqueeze(1).broadcast_to(
                [P, N_EDGE_TYPES, F_EDGE]), ALU.mult))
            done(v.tensor_reduce(type_score[:], emb_act[:], AX.X, ALU.add))

            before = steps[0]
            STEPS = 18
            with dve.Fori(0, ITERS) as i:
                for u in range(U):
                    c = i * U + u
                    at = i * (U * STEPS)
                    m = meta_sb[u]
                    dve.wait_ge(hib_in[u], (i + 1) * 16)
                    dve.wait_ge(pick_mm, count(c * TG))
                    v.tensor_scalar(onehot[:], hib_sb[u][:], part[:, 0:1], None, ALU.is_equal).then_inc(
                        onehot_ready, 1)
                    dve.wait_ge(eae_scaled, c + 1)
                    dve.wait_ge(msg_mm, count(c))
                    v.tensor_tensor(eae[:], eae_s[:], ps_attr[0:G * F_EDGE, :, 0:TG * P // 2], ALU.max).then_inc(
                        eae_ready, 1)
                    dve.wait_ge(meta_in[u], (i + 1) * 16)
                    done(v.tensor_copy(dstc[:], m[:, T:2 * T + 1]), at)
                    div98(hic[:], dstc[:, 1:T + 1], at)
                    done(v.scalar_tensor_tensor(loc[:], hic[:], -float(NPP), dstc[:, 1:T + 1], ALU.mult, ALU.add), at)
                    done(v.tensor_tensor(pen[:], dstc[:, 1:T + 1], dstc[:, 0:T], ALU.is_equal), at)
                    done(v.tensor_scalar(pen[:], pen[:], BIG, BIG, ALU.mult, ALU.subtract), at)
                    done(v.tensor_copy(etc[:], m[:, 2 * T + 1:3 * T + 1]), at)
                    done(v.tensor_tensor(emask[:], etc[:].unsqueeze(2).broadcast_to([P, T, N_EDGE_TYPES]),
                                         types8[:].unsqueeze(1).broadcast_to([P, T, N_EDGE_TYPES]), ALU.is_equal), at)
                    done(v.tensor_tensor(emask[:], emask[:], type_score[:].unsqueeze(1).broadcast_to(
                        [P, T, N_EDGE_TYPES]), ALU.mult), at)
                    done(v.tensor_reduce(escore[:], emask[:], AX.X, ALU.add), at)
                    for t in range(T):
                        g, j = t // G, t % G
                        if j == 0:
                            dve.wait_ge(pick_mm, count(c * TG + g + 1))
                        v.scalar_tensor_tensor(pick[:, t, :], free98[:], loc[:, t:t + 1],
                                               ps_pick[:, g % 2, j * NPP:(j + 1) * NPP], ALU.is_equal, ALU.mult,
                                               accum_out=dscore[:, t:t + 1]).then_inc(picked, 1)
                    dve.wait_ge(picked, count((c + 1) * T))
                    done(v.tensor_tensor(escore[:], escore[:], dscore[:], ALU.add), at)
                    dve.wait_ge(gathered[u], (i + 1) * (16 * T))
                    dve.wait_ge(msg_mm, count(c + 1))
                    v.tensor_tensor(msg[:, 0:3 * G, :], gath[u][:, 0:3 * G, 0:VW],
                                    ps_msg[:, 0, 0:3 * G * VW].rearrange("p (t f) -> p t f", f=VW), ALU.add)
                    v.tensor_tensor(msg[:, 3 * G:T, :], gath[u][:, 3 * G:T, 0:VW],
                                    ps_msg[:, 1, 0:2 * G * VW].rearrange("p (t f) -> p t f", f=VW),
                                    ALU.add).then_inc(msg_added, 1)
                    dve.wait_ge(msg_added, count(c + 1))
                    done(v.tensor_tensor(alpha[:], msg[:, :, F_IN], escore[:], ALU.add), at)
                    done(v.scalar_tensor_tensor(alpha[:], alpha[:], SLOPE, alpha[:], ALU.mult, ALU.max), at)
                    done(v.tensor_copy(mrun[:, 0:1], mrun[:, T:T + 1]), at)
                    done(v.tensor_tensor_scan(mrun[:, 1:T + 1], pen[:], alpha[:], mrun[:, 0:1], ALU.add, ALU.max), at)
                    v.tensor_tensor(args[:, 0, :], alpha[:], mrun[:, 1:T + 1], ALU.subtract)
                    done(v.tensor_tensor(args[:, 1, :], mrun[:, 0:T], pen[:], ALU.add), at)
                    v.tensor_tensor(args[:, 1, :], args[:, 1, :], mrun[:, 1:T + 1], ALU.subtract).then_inc(
                        args_ready, 1)
                    done(v.tensor_copy(terms[:, :, 0:1], sums[:, :, T:T + 1]), at)
                    dve.wait_ge(exp_done, c + 1)
                    v.tensor_copy(terms[:, F_IN, 1:T + 1], wts[:, 0, :])
                    done(v.tensor_tensor(terms[:, 0:F_IN, 1:T + 1].rearrange("p f t -> p t f"), msg[:, :, 0:F_IN],
                                         wts[:, 0, :].unsqueeze(2).broadcast_to([P, T, F_IN]), ALU.mult), at)
                    dve.wait_ge(keep_ready, c + 1)
                    dve.wait_ge(rows_sums, count(c))
                    v.tensor_tensor_scan(sums[:].rearrange("p f t -> p (f t)"), keep[:].rearrange("p f t -> p (f t)"),
                                         terms[:].rearrange("p f t -> p (f t)"), 0.0, ALU.mult,
                                         ALU.add).then_inc(sums_ready, 1)
                    dve.wait_ge(sums_ready, count(c + 1))
            assert steps[0] == before + U * STEPS
            steps[0] = before + U * STEPS * ITERS

            done(v.tensor_copy(blk_last[:], blk_last_i[:]))
            base = steps[0]
            with dve.Fori(0, NODE_ITERS) as i:
                for j in range(N7):
                    at = i * N7
                    done(v.tensor_scalar(cnt_tmp[:], blk_last[:], node_id[:, ds(i * N7 + j, 1)], 0.0, ALU.is_le, ALU.add,
                                         accum_out=nblk[:, ds(i * N7 + j, 1)]), at)
                    v.tensor_scalar(blk_idx[j][:], nblk[:, ds(i * N7 + j, 1)], float(NBLK - 1), None,
                                    ALU.min).then_inc(blk_idx_ready, 1)
                for j in range(N7):
                    dve.wait_ge(blk_in[j], (i + 1) * 16)
                    last = v.tensor_scalar(blk[j], blk[j], node_id[:, ds(i * N7 + j, 1)], 0.0, ALU.is_le,
                                           ALU.add, accum_out=incnt[:, ds(i * N7 + j, 1)])
                last.then_inc(blk_counted, 1)
            steps[0] = base + N7 * NODE_ITERS
            dve.wait_ge(blk_counted, NODE_ITERS)
            done(v.tensor_scalar(nblk[:], nblk[:], float(NBLK - 1), None, ALU.min))
            done(v.scalar_tensor_tensor(nblk[:], nblk[:], float(BLK), incnt[:], ALU.mult, ALU.add))
            done(v.tensor_scalar(nblk[:], nblk[:], -1.0, 0.0, ALU.add, ALU.max))
            done(v.tensor_copy(pos[:], nblk[:]))

            done(v.tensor_copy(redge[:], redge_i[:]))
            done(v.tensor_copy(rlast[:], rlast_i[:]))
            done(v.tensor_scalar(hi_f[:], dst_f[:], redge[:, 0:1], 0.0, ALU.is_equal, ALU.add, accum_out=head[:, 0:1]))
            done(v.scalar_tensor_tensor(head[:, 1:2], part[:], float(EPP), head[:, 0:1], ALU.mult, ALU.add))
            done(v.tensor_scalar(head[:, 1:2], head[:, 1:2], -1.0, None, ALU.add))
            done(v.tensor_tensor(head[:, 2:3], redge[:, 0:1], redge[:, 2:3], ALU.is_equal))
            done(v.tensor_tensor(head[:, 3:4], redge[:, 1:2], redge[:, 3:4], ALU.is_equal))
            done(v.scalar_tensor_tensor(head[:, 3:4], head[:, 0:1], float(EPP), head[:, 3:4], ALU.is_equal, ALU.mult))
            done(v.scalar_tensor_tensor(head[:, 4:5], head[:, 3:4], 0.0, head[:, 2:3], ALU.is_equal, ALU.mult))
            done(v.tensor_scalar(head[:, 5:6], head[:, 4:5], -float(2 ** 21), float(2 ** 21), ALU.mult, ALU.add))
            done(v.tensor_tensor(head[:, 5:6], head[:, 5:6], head[:, 1:2], ALU.add))
            done(v.tensor_copy(head_idx[:, 0:1], head[:, 1:2]))
            done(v.tensor_copy(head_idx[:, 1:2], head[:, 5:6]))
            done(v.tensor_scalar(contrib[:], free128[:], part[:, 0:1], None, ALU.is_lt))
            done(v.scalar_tensor_tensor(contrib[:], rlast[:], redge[:, 0:1], contrib[:], ALU.is_equal, ALU.mult))
            dve.wait_ge(tails_in, 16)
            v.tensor_copy(mtail[:], tails[:, VW:VW + 1].broadcast_to([P, P])).then_inc(head_idx_ready, 1)
            dve.wait_ge(mtail_mm, 1)
            done(v.tensor_tensor(mtail[:], ps_misc[:, 0, 0:P], contrib[:], ALU.mult))
            done(v.tensor_scalar(wtailT[:], contrib[:], BIG, BIG, ALU.mult, ALU.subtract))
            done(v.tensor_tensor(mtail[:], mtail[:], wtailT[:], ALU.add))
            done(v.tensor_reduce(fix[:, 0:1], mtail[:], AX.X, ALU.max))
            dve.wait_ge(own_in, 16)
            done(v.tensor_tensor(fix[:, 0:1], fix[:, 0:1], own[:, VW:VW + 1], ALU.max))
            done(v.tensor_tensor(fix[:, 1:2], own[:, VW:VW + 1], fix[:, 0:1], ALU.subtract))
            v.tensor_scalar(mtail[:], mtail[:], fix[:, 0:1], None, ALU.subtract).then_inc(targs_ready, 1)
            dve.wait_ge(wtailT_mm, 1)
            v.tensor_copy(wtailT[:], ps_misc[:, 0, P:2 * P]).then_inc(wtailT_sb, 1)
            v.tensor_copy(joined[:, VW:VW + 1], fix[:, 0:1])
            v.tensor_copy(joined[:, VW + 1:RW], own[:, VW + 1:RW])
            dve.wait_ge(tsum_mm, 1)
            v.scalar_tensor_tensor(joined[:, 0:VW], own[:, 0:VW], fix[:, 2:3], ps_misc[:, 0, 2 * P:2 * P + VW],
                                   ALU.mult, ALU.add).then_inc(joined_ready, 1)
            dve.wait_ge(last_in, 16 * NPP)
            done(v.tensor_tensor(scale[:, 0, :], last_rows[:, :, VW + 1], node_id[:], ALU.is_equal))
            done(v.tensor_scalar(scale[:, 1, :], last_rows[:, :, F_IN], 1e-16, None, ALU.add))
            done(v.reciprocal(scale[:, 1, :], scale[:, 1, :]))
            done(v.tensor_tensor(scale[:, 0, :], scale[:, 0, :], scale[:, 1, :], ALU.mult))
            done(v.tensor_tensor(h[:], last_rows[:, :, 0:F_IN], scale[:, 0, :].unsqueeze(2).broadcast_to(
                [P, NPP, F_IN]), ALU.mult))
            v.tensor_tensor(h[:], h[:], x_sb[:], ALU.add).then_inc(out_ready, 1)


def kernel(x, src, dst, edge_attr_16, edge_type_8, node_type_4, L0_gnn_hetero_w, L0_gnn_hetero_b,
           L0_gnn_edge_type_emb, L0_gnn_edge_attr_w, L0_gnn_att_w, L0_gnn_lin_w):
    import numpy as np
    import concourse.bacc as bacc
    from concourse.bass_utils import run_bass_kernel_spmd

    x, src, dst = np.asarray(x), np.asarray(src), np.asarray(dst)
    node_type, edge_type = np.asarray(node_type_4), np.asarray(edge_type_8)
    pad = N_PAD - N_NODES
    rows = dst.reshape(P, EPP)
    before = np.full((P, 1), -1, dst.dtype)
    dst_prev = np.concatenate([before, rows], axis=1)
    windows = np.stack([dst_prev[:, c * T:(c + 1) * T + 1] for c in range(CHUNKS)], axis=1)
    meta = np.concatenate([src.reshape(P, CHUNKS, T), windows, edge_type.reshape(P, CHUNKS, T)], axis=2)
    none = np.full((1,), -1, dst.dtype)
    row_edges = np.stack([rows[:, 0], rows[:, -1], np.concatenate([none, rows[:-1, -1]]),
                          np.concatenate([rows[1:, 0], none])], axis=1)
    attr = np.asarray(edge_attr_16).reshape(P, CHUNKS, TG, G, F_EDGE).transpose(3, 4, 1, 2, 0)
    arrays = {
        "x_in": np.concatenate([x, np.zeros((pad, F_IN), x.dtype)]).reshape(P, NPP, F_IN),
        "meta_in": meta,
        "dst_rows_in": rows,
        "dst_tmajor_in": rows.T.reshape(P, EPP),
        "dst_last_of_block_in": dst[BLK - 1::BLK],
        "row_edges_in": row_edges,
        "row_last_in": rows[:, -1],
        "edge_attr_t_in": attr.reshape(G * F_EDGE, CHUNKS, TG * P),
        "node_type_in": np.concatenate([node_type, np.zeros((pad,), node_type.dtype)]).reshape(P, NPP),
        "hetero_wT_in": np.asarray(L0_gnn_hetero_w).transpose(2, 0, 1).reshape(F_IN, N_NODE_TYPES * F_IN),
        "hetero_bT_in": np.asarray(L0_gnn_hetero_b).T,
        "edge_type_emb_in": np.asarray(L0_gnn_edge_type_emb),
        "edge_attr_w_in": np.asarray(L0_gnn_edge_attr_w),
        "att_w_in": np.asarray(L0_gnn_att_w),
        "lin_w_in": np.asarray(L0_gnn_lin_w),
    }
    nc = bacc.Bacc("TRN2", target_bir_lowering=False, num_devices=1)
    args = []
    for name in list(arrays):
        arrays[name] = np.ascontiguousarray(arrays[name])
        args.append(nc.dram_tensor(name, arrays[name].shape, mybir.dt.from_np(arrays[name].dtype),
                                   kind="ExternalInput").ap())
    out = nc.dram_tensor("out_dram", (P, NPP, F_IN), mybir.dt.float32, kind="ExternalOutput").ap()
    gnn_kernel(nc, *args, out)
    result = run_bass_kernel_spmd(nc, [arrays], core_ids=[0])
    return result.results[0]["out_dram"].reshape(N_PAD, F_IN)[:N_NODES]
```

```python
import concourse.bass as bass
from concourse import mybir
from contextlib import ExitStack

N_NODES = 12500
N_EDGES = 400000
F_IN = 32
F_EDGE = 16
N_NODE_TYPES = 4
N_EDGE_TYPES = 8
SLOPE = 0.2

P = 128
EPP = N_EDGES // P
NPP = -(-N_NODES // P)
N_PAD = P * NPP
T = 25
CHUNKS = EPP // T
U = 5
ITERS = CHUNKS // U
TS = 3
TD = T - TS
SEL = CHUNKS * TS
G = 5
TG = T // G
YW = F_IN + 2
NG = 7
GN = NPP // NG
VW = F_IN + 1
RW = F_IN + 3
META = 3 * T + 1
BIG = 3.0e38
ROUND = 12582912.0
N7 = 7
NODE_ITERS = NPP // N7
WARM_UP = 14
MB = N7 * N_NODE_TYPES


def gnn_kernel(nc, x, meta, dst_rows, dst_tmajor, sel_src, row_edges, row_last, edge_attr_t, node_type,
               hetero_wT, hetero_bT, edge_type_emb, edge_attr_w, att_w, lin_w, out):
    fp32, bf16, i32 = mybir.dt.float32, mybir.dt.bfloat16, mybir.dt.int32
    ALU, ACT, AX = mybir.AluOpType, mybir.ActivationFunctionType, mybir.AxisListType
    ds = bass.ds

    table_dram = nc.dram_tensor("table_dram", (N_PAD, YW), fp32, kind="Internal").ap()
    dst_hi_dram = nc.dram_tensor("dst_hi_dram", (CHUNKS, T * P), bf16, kind="Internal").ap()
    sel_code_dram = nc.dram_tensor("sel_code_dram", (CHUNKS, TS * P), mybir.dt.float16, kind="Internal").ap()
    rows_dram = nc.dram_tensor("rows_dram", (N_EDGES + N_PAD, RW), fp32, kind="Internal").ap()
    rows_pm = rows_dram[0:N_EDGES, :].rearrange("(p e) f -> p e f", p=P)
    rows_after = rows_dram[1:N_EDGES + 1, :].rearrange("(p e) f -> p e f", p=P)
    node_rows = rows_dram[N_EDGES:N_EDGES + N_PAD, :].rearrange("(p n) f -> p n f", p=P)

    ctx = ExitStack()
    with ctx:
        def sb(name, shape, dt=fp32):
            return ctx.enter_context(nc.sbuf_tensor(name, shape, dt))

        def sem(name):
            return ctx.enter_context(nc.semaphore(name))

        ident = sb("ident", [P, P])
        part = sb("part", [P, 1])
        free98 = sb("free98", [P, NPP])
        free128 = sb("free128", [P, P])
        half128 = sb("half128", [P, P])
        node_id = sb("node_id", [P, NPP])
        part_group = sb("part_group", [P, NG])
        group_row = sb("group_row", [MB, N7])
        group_sel = sb("group_sel", [MB, N7])
        types8 = sb("types8", [P, N_EDGE_TYPES])
        scores_w = sb("scores_w", [F_IN, YW])
        het_wT = sb("het_wT", [F_IN, P])
        het_bT = sb("het_bT", [F_IN, N_NODE_TYPES])
        node_w = sb("node_w", [P, YW])
        het_bT7 = sb("het_bT7", [F_IN, N7, N_NODE_TYPES])
        node_b = sb("node_b", [MB, YW])
        node_b7 = sb("node_b7", [MB, N7, YW])
        attr_w = sb("attr_w", [G * F_EDGE, G * F_EDGE])
        msg_w = sb("msg_w", [G * F_EDGE, G * VW])
        emb = sb("emb", [P, N_EDGE_TYPES, F_EDGE])
        emb_act = sb("emb_act", [P, N_EDGE_TYPES, F_EDGE])
        att_type = sb("att_type", [P, F_EDGE])
        type_score = sb("type_score", [P, N_EDGE_TYPES])

        parts = sb("parts", [P, 3, NG, VW * GN], bf16)
        x_sb = parts[:].rearrange("p k g m -> p (k g m)").bitcast(fp32)[:, 0:NPP * F_IN].rearrange(
            "p (n f) -> p n f", f=F_IN)
        h = sb("h", [P, NPP, F_IN])
        node_buf = sb("node_buf", [P, NPP * RW])
        table = node_buf[:, 0:NPP * YW].rearrange("p (n f) -> p n f", f=YW)
        last_rows = node_buf[:].rearrange("p (n f) -> p n f", f=RW)

        def in_node_buf(at, shape, parts=P):
            size = shape[0] * shape[1]
            return node_buf[0:parts, at:at + size].rearrange("p (a b) -> p a b", b=shape[1])
        stat = sb("stat", [P, 4, NPP])
        ntype = sb("ntype", [P, NPP], i32)
        ntype_f = sb("ntype_f", [P, NPP])
        tmask = sb("tmask", [P, NPP, N_NODE_TYPES])
        hm = [sb(f"hm{k}", [P, N7, P]) for k in range(2)]
        hmask = [sb(f"hmask{k}", [P, MB]) for k in range(2)]
        hmT = [sb(f"hmT{k}", [P, N7 * P]) for k in range(2)]
        maskT = [sb(f"maskT{k}", [MB, P]) for k in range(2)]
        s_rest = sb("s_rest", [P, NPP])
        s_dst = sb("s_dst", [P, 3, NPP], bf16)

        dst_f = sb("dst_f", [P, EPP])
        hi_f = sb("hi_f", [P, EPP])
        dst_i = hi_f[:].bitcast(i32)
        meta_sb = [sb(f"meta{u}", [P, META], i32) for u in range(U)]
        attr_sb = [sb(f"attr{u}", [G * F_EDGE, TG * P]) for u in range(U)]
        hib_sb = [sb(f"hib{u}", [P, T * P], bf16) for u in range(U)]
        gath = [sb(f"gath{u}", [P, T, YW]) for u in range(U)]
        rows = [sb(f"rows{u}", [P, T, RW]) for u in range(U)]
        onehot = sb("onehot", [P, T * P], bf16)
        hi_b = onehot[:, 0:EPP]
        eae_s = in_node_buf(0, [2, TG * P // 2], G * F_EDGE)
        eae = in_node_buf(TG * P, [2, TG * P // 2], G * F_EDGE)
        dstc = [sb(f"dstc{u}", [P, T + 1]) for u in range(U)]
        hic = [sb(f"hic{u}", [P, T]) for u in range(U)]
        loc = [sb(f"loc{u}", [P, T]) for u in range(U)]
        sign_hi = hi_f[:, 0:T * P // 2].bitcast(bf16).rearrange("p (t m) -> p t m", m=P)
        sign_lo = hi_f[:, T * P // 2:T * (P + NPP) // 2].bitcast(bf16).rearrange("p (t m) -> p t m", m=NPP)
        pen = sb("pen", [P, T])
        etc = sb("etc", [P, T])
        emask = sb("emask", [P, T, N_EDGE_TYPES])
        escore = sb("escore", [P, T])
        pick = h[:].rearrange("p n f -> p (n f)")[:, 0:T * NPP].rearrange("p (t n) -> p t n", n=NPP)
        dscore = sb("dscore", [P, T])
        msg = in_node_buf(2 * TG * P, [T, VW])
        alpha = sb("alpha", [P, T])
        mrun = sb("mrun", [P, T + 1])
        args = sb("args", [P, 2, T])
        wts = sb("wts", [P, 2, T])
        terms = in_node_buf(2 * TG * P + T * VW, [VW, T + 1])
        keep = sb("keep", [P, VW, T + 1])
        sums = sb("sums", [P, VW, T + 1])
        sel_code = sb("sel_code", [P, SEL], mybir.dt.float16)
        sel_node = sb("sel_node", [P, SEL])
        code_sb = [dst_f[:, 4 * SEL + u * (TS * P // 2):4 * SEL + (u + 1) * (TS * P // 2)].bitcast(mybir.dt.float16)
                   for u in range(U)]
        sel_onehot = dst_f[:, 0:NG * TS * P // 2].bitcast(bf16).rearrange("p (g e) -> p g e", g=NG)
        sel_mask = sb("sel_mask", [P, TS, GN])
        sel_prod = h[:].rearrange("p n f -> p (n f)")[:, T * NPP:T * NPP + VW * GN].rearrange("p (f n) -> p f n", n=GN)
        sel_tmp = [h[:].rearrange("p n f -> p (n f)")[:, k * 2 * SEL:(k + 1) * 2 * SEL] for k in range(4)]

        differ = sb("differ", [P, P], bf16)
        sign_sums = sb("sign_sums", [P, NPP])
        sign_parts = sb("sign_parts", [P, 3, NPP], bf16)
        cnt = sb("cnt", [P, NPP])
        pos = sb("pos", [P, NPP], i32)
        redge_i = sb("redge_i", [P, 4], i32)
        redge = sb("redge", [P, 4])
        rlast_i = sb("rlast_i", [P, P], i32)
        rlast = sb("rlast", [P, P])
        head = sb("head", [P, 8])
        head_idx = sb("head_idx", [P, 2], i32)
        own = sb("own", [P, RW])
        tails = sb("tails", [P, RW])
        contrib = sb("contrib", [P, P])
        mtail = sb("mtail", [P, P])
        wtail = sb("wtail", [P, P])
        wtailT = sb("wtailT", [P, P])
        fix = sb("fix", [P, 4])
        joined = sb("joined", [P, RW])
        scale = sb("scale", [P, 2, NPP])

        falls = sb("falls", [P, 2])
        unsorted = sb("unsorted", [P, 1])
        unsorted_i = sb("unsorted_i", [P, 1], i32)
        before_me = sb("before_me", [P, P])
        tile_rows = sb("tile_rows", [P, RW])
        next_row = sb("next_row", [P, 2])
        mg = sb("mg", [P, 8])
        merge_idx = sb("merge_idx", [P, 2], i32)

        def bank(name, n=1):
            return ctx.enter_context(nc.psum_tensor(name, [P, n, 512], fp32))

        ps_attr = bank("ps_attr", 2)
        ps_msg = bank("ps_msg", 2)
        ps_pick = bank("ps_pick", 2)
        ps_misc = bank("ps_misc", 2)
        ps_sel = ps_misc
        ps_signs = ps_msg[:, 1, 2 * G * VW:2 * G * VW + NPP]
        ps_hmT = [ps_attr, ps_pick]

        weights_in = sem("weights_in")
        zeroed = sem("zeroed")
        diag_in = sem("diag_in")
        x_in = sem("x_in")
        dst_in = sem("dst_in")
        consts = sem("consts")
        dve_step = sem("dve_step")
        signs_ready = sem("signs_ready")
        signs_mm = sem("signs_mm")
        signs_summed = sem("signs_summed")
        places_ready = sem("places_ready")
        sign_parts_ready = sem("sign_parts_ready")
        differ_mm = sem("differ_mm")
        node_w_mm = sem("node_w_mm")
        node_w_sb = sem("node_w_sb")
        node_b7_ready = sem("node_b7_ready")
        maskT_sb = sem("maskT_sb")
        head_counted = sem("head_counted")
        var_ready = sem("var_ready")
        dev_ready = sem("dev_ready")
        zeros_ready = sem("zeros_ready")
        hm_ready = sem("hm_ready")
        hmT_mm = sem("hmT_mm")
        hmT_sb = sem("hmT_sb")
        tab_mm = sem("tab_mm")
        tab_sb = sem("tab_sb")
        table_out = sem("table_out")
        hi_ready = sem("hi_ready")
        hi_out = sem("hi_out")
        s_parts = sem("s_parts")
        sel_in = sem("sel_in")
        codes_ready = sem("codes_ready")
        codes_out = sem("codes_out")
        code_in = [sem(f"code_in{u}") for u in range(U)]
        sel_first_ready = sem("sel_first_ready")
        sel_onehot_ready = sem("sel_onehot_ready")
        parts_ready = sem("parts_ready")
        sel_mm = sem("sel_mm")
        sel_read = sem("sel_read")
        gather_turns = sem("gather_turns")
        meta_in = [sem(f"meta_in{u}") for u in range(U)]
        attr_in = [sem(f"attr_in{u}") for u in range(U)]
        hib_in = [sem(f"hib_in{u}") for u in range(U)]
        gathered = [sem(f"gathered{u}") for u in range(U)]
        stored = [sem(f"stored{u}") for u in range(U)]
        attr_mm = sem("attr_mm")
        eae_scaled = sem("eae_scaled")
        eae_ready = sem("eae_ready")
        msg_mm = sem("msg_mm")
        msg_added = sem("msg_added")
        onehot_ready = sem("onehot_ready")
        pick_mm = sem("pick_mm")
        picked = sem("picked")
        args_ready = sem("args_ready")
        exp_done = sem("exp_done")
        keep_ready = sem("keep_ready")
        sums_ready = sem("sums_ready")
        rows_sums = sem("rows_sums")
        head_idx_ready = sem("head_idx_ready")
        own_in = sem("own_in")
        tails_in = sem("tails_in")
        mtail_mm = sem("mtail_mm")
        targs_ready = sem("targs_ready")
        texp_done = sem("texp_done")
        wtailT_mm = sem("wtailT_mm")
        wtailT_sb = sem("wtailT_sb")
        tsum_mm = sem("tsum_mm")
        joined_ready = sem("joined_ready")
        falls_ready = sem("falls_ready")
        falls_mm = sem("falls_mm")
        unsorted_ready = sem("unsorted_ready")
        pos_ready = sem("pos_ready")
        join_step = sem("join_step")
        merge_step = sem("merge_step")
        last_step = sem("last_step")
        node_rows_ready = sem("node_rows_ready")
        node_rows_out = sem("node_rows_out")
        sp_turns = sem("sp_turns")
        tile_in = sem("tile_in")
        merge_keys = sem("merge_keys")
        merge_keys_mm = sem("merge_keys_mm")
        merge_idx_ready = sem("merge_idx_ready")
        node_in = sem("node_in")
        merge_args = sem("merge_args")
        merge_exp = sem("merge_exp")
        merge_wT_mm = sem("merge_wT_mm")
        merge_wT_sb = sem("merge_wT_sb")
        merge_sum_mm = sem("merge_sum_mm")
        merge_row_ready = sem("merge_row_ready")
        merge_out = sem("merge_out")
        joined_out = sem("joined_out")
        last_in = sem("last_in")
        out_ready = sem("out_ready")
        out_done = sem("out_done")

        def count(n):
            return n + 1

        def start_at_one(eng, *sems):
            for s in sems:
                eng.sem_inc(s, 1)

        def is_unsorted(eng):
            eng.wait_ge(unsorted_ready, 1)
            return eng.value_load(unsorted_i[0:1, 0:1], min_val=0, max_val=1)

        block = ctx.enter_context(nc.Block())

        @block.sync
        def _(sp):
            def load_hib(c, u):
                sp.dma_start(hib_sb[u][:], dst_hi_dram[ds(c, 1), :].rearrange("a e -> (a e)")
                             .partition_broadcast(P)).then_inc(hib_in[u], 16)

            def load_code(c, u):
                sp.dma_start(code_sb[u], sel_code_dram[ds(c, 1), :].rearrange("a e -> (a e)")
                             .partition_broadcast(P)).then_inc(code_in[u], 16)

            def load_attr(c, u):
                sp.dma_start(attr_sb[u][:], edge_attr_t[:, ds(c, 1), :].rearrange("k a m -> k (a m)")).then_inc(
                    attr_in[u], 16)

            sp.dma_start(x_sb, x).then_inc(x_in, 16)
            sp.dma_start(ntype[:], node_type).then_inc(x_in, 16)
            for dst, src in ((scores_w[:, 0:F_IN], lin_w[0:F_IN, :]),
                             (scores_w[:, F_IN:F_IN + 1], att_w[F_IN:2 * F_IN, :]),
                             (scores_w[:, F_IN + 1:F_IN + 2], att_w[0:F_IN, :]),
                             (het_wT[:], hetero_wT), (het_bT[:], hetero_bT),
                             (emb[:], edge_type_emb.partition_broadcast(P)),
                             (att_type[:], att_w[2 * F_IN:2 * F_IN + F_EDGE, 0].partition_broadcast(P)),
                             (redge_i[:], row_edges), (rlast_i[:], row_last.partition_broadcast(P))):
                sp.dma_start(dst, src).then_inc(weights_in, 16)
            sp.dma_start(dst_i, dst_tmajor).then_inc(dst_in, 16)
            for u in range(U):
                sp.dma_start(meta_sb[u][:], meta[:, u, :]).then_inc(meta_in[u], 16)
            sp.wait_ge(zeroed, 2)
            for g in range(G):
                k = slice(g * F_EDGE, (g + 1) * F_EDGE)
                sp.dma_start(attr_w[k, k], edge_attr_w).then_inc(diag_in, 16)
                sp.dma_start(msg_w[k, g * VW:g * VW + F_IN], lin_w[F_IN:F_IN + F_EDGE, :]).then_inc(diag_in, 16)
                sp.dma_start(msg_w[k, g * VW + F_IN:(g + 1) * VW],
                             att_w[2 * F_IN + F_EDGE:2 * F_IN + 2 * F_EDGE, :]).then_inc(diag_in, 16)
            for u in range(U):
                load_attr(u, u)
            sp.wait_ge(tab_sb, NODE_ITERS + 2)
            sp.dma_start(table_dram.rearrange("(p n) f -> p n f", p=P), table).then_inc(table_out, 16)
            sp.wait_ge(hi_ready, 1)
            sp.dma_start(dst_hi_dram.rearrange("c (a b) -> (c a b)", a=1).rearrange("(p e) -> p e", p=P),
                         hi_b).then_inc(hi_out, 16)
            sp.dma_start(sel_tmp[0].bitcast(i32), sel_src).then_inc(sel_in, 16)
            sp.dma_start(dst_i, dst_rows).then_inc(dst_in, 16)
            sp.wait_ge(hi_out, 16)
            for u in range(U):
                load_hib(u, u)
            sp.wait_ge(codes_ready, 1)
            sp.dma_start(sel_code_dram.rearrange("c (a b) -> (c a b)", a=1).rearrange("(p e) -> p e", p=P),
                         sel_code[:]).then_inc(codes_out, 16)
            sp.wait_ge(codes_out, 16)
            sp.wait_ge(head_counted, 1)
            for u in range(U):
                load_code(u, u)
            sp.wait_ge(node_rows_ready, 1)
            sp.dma_start(node_rows, last_rows).then_inc(node_rows_out, 16)
            with sp.Fori(1, ITERS) as i:
                for u in range(U):
                    sp.wait_ge(sums_ready, count(i * U + u + 1 - U))
                    sp.dma_start(meta_sb[u][:], meta[:, ds(i * U + u, 1), :].rearrange("p a m -> p (a m)")).then_inc(
                        meta_in[u], 16)
                    load_hib(i * U + u, u)
                    load_code(i * U + u, u)
                    load_attr(i * U + u, u)
            for u in range(U):
                sp.wait_ge(stored[u], 16 * ITERS + 1)
            flag = is_unsorted(sp)
            sp.wait_ge(sel_mm, count(SEL))
            sp.dma_start(x_sb, x).then_inc(x_in, 16)
            with sp.If(flag < 1):
                sp.dma_start(tails[:], rows_pm[:, EPP - 1, :]).then_inc(tails_in, 16)
                sp.wait_ge(tails_in, 16)
            with sp.If(flag >= 1):
                sp.wait_ge(node_rows_out, 16)
                with sp.Fori(0, EPP) as t:
                    sp.dma_start(tile_rows[:], rows_pm[:, ds(t, 1), :].rearrange("p a f -> p (a f)")).then_inc(
                        tile_in, 16)
                    sp.dma_start(next_row[:], rows_after[:, ds(t, 1), VW:RW].rearrange("p a f -> p (a f)")).then_inc(tile_in, 16)
                    sp.wait_ge(merge_row_ready, t + 1)
                    sp.sem_inc(sp_turns, 1)
            sp.wait_ge(out_ready, 1)
            sp.dma_start(out, h[:]).then_inc(out_done, 16)
            sp.wait_ge(out_done, 16)
            sp.wait_ge(table_out, 16)

        @block.gpsimd
        def _(pool):
            nc.gpsimd.memset(attr_w[:], 0.0).then_inc(zeroed, 1)
            nc.gpsimd.memset(msg_w[:], 0.0).then_inc(zeroed, 1)
            nc.gpsimd.memset(ident[:], 0.0).then_inc(consts, 1)
            pool.wait_ge(consts, 1)
            nc.gpsimd.affine_select(out=ident[:], in_=ident[:], compare_op=ALU.not_equal, fill=1.0, base=0,
                                    pattern=[[-1, P]], channel_multiplier=1).then_inc(consts, 1)
            for tile, base, step, mult in ((part, 0, 0, 1), (free98, 0, 1, 0), (free128, 0, 1, 0),
                                           (node_id, 0, 1, NPP), (types8, 0, 1, 0),
                                           (group_row, 0, -N_NODE_TYPES, 1),
                                           (part_group, 0, P, 1)):
                nc.gpsimd.iota(tile[:], [[step, tile.shape[1]]], base=base, channel_multiplier=mult,
                               allow_small_or_imprecise_dtypes=True).then_inc(consts, 1)
            pool.wait_ge(table_out, 16)
            with pool.Fori(0, ITERS) as i:
                for u in range(U):
                    pool.wait_ge(meta_in[u], (i + 1) * 16)
                    pool.sem_inc(gather_turns, 1)
                    for t in range(TD):
                        nc.gpsimd.indirect_dma_start(
                            gath[u][:, t, :], None, table_dram,
                            bass.IndirectOffsetOnAxis(ap=meta_sb[u][:, t:t + 1], axis=0)).then_inc(gathered[u], 16)
            for u in range(U):
                pool.wait_ge(stored[u], 16 * ITERS + 1)
            flag = is_unsorted(pool)
            with pool.If(flag < 1):
                pool.wait_ge(head_idx_ready, 1)
                nc.gpsimd.indirect_dma_start(own[:], None, rows_dram,
                                             bass.IndirectOffsetOnAxis(ap=head_idx[:, 0:1], axis=0)).then_inc(own_in, 16)
                pool.wait_ge(joined_ready, 1)
                nc.gpsimd.indirect_dma_start(rows_dram, bass.IndirectOffsetOnAxis(ap=head_idx[:, 1:2], axis=0),
                                             joined[:], None, bounds_check=N_EDGES - 1, oob_is_err=False).then_inc(
                    joined_out, 16)
                pool.wait_ge(joined_out, 16)
            with pool.If(flag >= 1):
                pool.wait_ge(node_rows_out, 16)
                with pool.Fori(0, EPP) as t:
                    pool.wait_ge(merge_idx_ready, t + 1)
                    pool.sem_inc(gather_turns, 1)
                    nc.gpsimd.indirect_dma_start(
                        own[:], None, rows_dram,
                        bass.IndirectOffsetOnAxis(ap=merge_idx[:, 0:1], axis=0)).then_inc(node_in, 16)
                    pool.wait_ge(merge_row_ready, t + 1)
                    pool.sem_inc(gather_turns, 1)
                    nc.gpsimd.indirect_dma_start(
                        rows_dram, bass.IndirectOffsetOnAxis(ap=merge_idx[:, 1:2], axis=0), joined[:], None,
                        bounds_check=N_EDGES + N_PAD - 1, oob_is_err=False).then_inc(merge_out, 16)
                    pool.wait_ge(merge_out, t * 16 + 16)
                    pool.sem_inc(gather_turns, 1)
            pool.wait_ge(pos_ready, 1)
            pool.wait_ge(node_rows_out, 16)
            for n in range(NPP):
                nc.gpsimd.indirect_dma_start(
                    last_rows[:, n, :], None, rows_dram,
                    bass.IndirectOffsetOnAxis(ap=pos[:, n:n + 1], axis=0)).then_inc(last_in, 16)

        @block.scalar
        def _(act):
            start_at_one(act, hmT_sb, rows_sums, *stored)
            act.wait_ge(node_w_mm, 1)
            nc.scalar.copy(node_w[:], ps_misc[:, 0, 0:YW])
            nc.scalar.copy(node_b[:], ps_misc[0:MB, 0, YW:2 * YW]).then_inc(node_w_sb, 1)
            act.wait_ge(var_ready, 1)
            nc.scalar.sqrt(stat[:, 3, :], stat[:, 2, :]).then_inc(dev_ready, 1)
            with act.Fori(0, NODE_ITERS // 2) as i:
                for k in range(2):
                    n = i * 2 + k
                    act.wait_ge(hmT_mm, n + 1)
                    act.wait_ge(tab_mm, n + 1)
                    for b, w in enumerate((4 * P, 3 * P)):
                        last = nc.scalar.copy(hmT[k][:, b * 4 * P:b * 4 * P + w], ps_hmT[k][:, b, 0:w])
                    last.then_inc(hmT_sb, 1)
            act.wait_ge(head_counted, 1)
            act.wait_ge(node_rows_out, 16)

            def scale_attr(c):
                act.wait_ge(attr_mm, c + 1)
                act.wait_ge(eae_ready, count(c))
                nc.scalar.mul(eae_s, ps_attr[0:G * F_EDGE, :, 0:TG * P // 2], SLOPE).then_inc(eae_scaled, 1)

            def chunk(i, u, final):
                c = i * U + u
                act.wait_ge(places_ready, c + 1)
                act.wait_ge(signs_mm, count(c))
                for t in range(T):
                    nc.scalar.activation(sign_hi[:, t, :], half128[:], ACT.Sign, bias=hic[u][:, t:t + 1],
                                         scale=-1.0)
                    last = nc.scalar.activation(sign_lo[:, t, :], half128[:, 0:NPP], ACT.Sign,
                                                bias=loc[u][:, t:t + 1], scale=-1.0)
                last.then_inc(signs_ready, 1)
                act.wait_ge(args_ready, c + 1)
                nc.scalar.activation(wts[:], args[:], ACT.Exp).then_inc(exp_done, 1)
                act.wait_ge(stored[u], i * 16 + 1)
                nc.scalar.copy(rows[u][:, :, VW], mrun[:, 1:T + 1])
                nc.scalar.copy(rows[u][:, :, VW + 1], dstc[u][:, 1:T + 1])
                act.wait_ge(exp_done, c + 1)
                act.wait_ge(sums_ready, count(c))
                nc.scalar.copy(keep[:, :, 1:T + 1], wts[:, 1:2, :].broadcast_to([P, VW, T])).then_inc(
                    keep_ready, 1)
                if not final:
                    scale_attr(c + 1)
                act.wait_ge(sums_ready, count(c + 1))
                nc.scalar.copy(rows[u][:, :, 0:VW], sums[:, :, 1:T + 1].rearrange("p f t -> p t f")).then_inc(
                    rows_sums, 1)
                act.wait_ge(rows_sums, count(c + 1))
                act.dma_start(rows_pm[:, ds(c * T, T), :], rows[u][:]).then_inc(stored[u], 16)

            scale_attr(0)
            with act.Fori(0, ITERS - 1) as i:
                for u in range(U):
                    chunk(i, u, False)
            for u in range(U):
                chunk(ITERS - 1, u, u == U - 1)
            flag = is_unsorted(act)
            with act.If(flag < 1):
                act.wait_ge(targs_ready, 1)
                nc.scalar.activation(wtail[:], mtail[:], ACT.Exp)
                nc.scalar.activation(fix[:, 2:3], fix[:, 1:2], ACT.Exp).then_inc(texp_done, 1)
            with act.If(flag >= 1):
                with act.Fori(0, EPP) as t:
                    act.wait_ge(merge_args, t + 1)
                    nc.scalar.activation(wtail[:], mtail[:], ACT.Exp)
                    nc.scalar.activation(fix[:, 2:3], fix[:, 1:2], ACT.Exp).then_inc(merge_exp, 1)

        @block.tensor
        def _(pe):
            pe.sem_inc(tab_mm, 2)
            start_at_one(pe, pick_mm, msg_mm, sel_mm, signs_mm)
            pe.wait_ge(weights_in, 9 * 16)
            nc.tensor.matmul(ps_misc[:, 0, 0:YW], het_wT[:], scores_w[:], start=True, stop=True)
            pe.wait_ge(node_b7_ready, 1)
            nc.tensor.matmul(ps_misc[0:MB, 0, YW:2 * YW], het_bT7[:].rearrange("f a b -> f (a b)"), scores_w[:],
                             start=True, stop=True).then_inc(node_w_mm, 1)
            pe.wait_ge(consts, 2)
            pe.wait_ge(node_w_sb, 1)
            pe.wait_ge(node_b7_ready, 2)

            def transposes(n, k):
                pe.wait_ge(hm_ready, n + 1)
                if not isinstance(n, int) or n:
                    pe.wait_ge(hmT_sb, n)
                    pe.wait_ge(maskT_sb, n)
                nc.tensor.transpose(ps_msg[0:MB, k, 0:P], hmask[k][:], ident[:])
                for j in range(N7):
                    last = nc.tensor.transpose(ps_hmT[k][:, j // 4, j % 4 * P:(j % 4 + 1) * P], hm[k][:, j, :],
                                               ident[:])
                last.then_inc(hmT_mm, 1)

            def products(n, k):
                pe.wait_ge(hmT_sb, count(n + 1))
                pe.wait_ge(maskT_sb, count(n + 1))
                pe.wait_ge(tab_sb, n + 1)
                nc.tensor.matmul(ps_misc[:, k, 0:N7 * YW], maskT[k][:], node_b7[:].rearrange("p a b -> p (a b)"),
                                 start=True, stop=False)
                for j in range(N7):
                    last = nc.tensor.matmul(ps_misc[:, k, j * YW:(j + 1) * YW], hmT[k][:, j * P:(j + 1) * P],
                                            node_w[:], start=False, stop=(j == N7 - 1))
                last.then_inc(tab_mm, 1)

            pe.wait_ge(zeros_ready, 1)
            pe.wait_ge(dev_ready, 1)
            zeros = sums[:].rearrange("p f t -> p (f t)").bitcast(bf16)
            for _ in range(WARM_UP):
                nc.tensor.matmul(ps_pick[:, 0, 0:512], zeros[:, 0:P], zeros[:, 0:512], start=True, stop=True)

            transposes(0, 0)
            with pe.Fori(0, NODE_ITERS // 2 - 1) as i:
                transposes(i * 2 + 1, 1)
                products(i * 2, 0)
                transposes(i * 2 + 2, 0)
                products(i * 2 + 1, 1)
            transposes(NODE_ITERS - 1, 1)
            products(NODE_ITERS - 2, 0)
            products(NODE_ITERS - 1, 1)
            pe.wait_ge(falls_ready, 1)
            nc.tensor.matmul(ps_misc[:, 0, 0:1], before_me[:], falls[:, 0:1], start=True, stop=True).then_inc(
                falls_mm, 1)
            pe.wait_ge(s_parts, 1)
            pe.wait_ge(diag_in, 3 * G * 16)

            def select(c, j):
                pe.wait_ge(sel_onehot_ready if j else sel_first_ready, c + 1)
                pe.wait_ge(sel_read, count(c * TS + (j - 1 if j > 1 else 0)))
                for g in range(NG):
                    for k in range(3):
                        last = nc.tensor.matmul(ps_sel[:, j % 2, 0:VW * GN], sel_onehot[:, g, j * P:(j + 1) * P],
                                                parts[:, k, g, :], start=(g == 0 and k == 0),
                                                stop=(g == NG - 1 and k == 2))
                last.then_inc(sel_mm, 1)

            def dst_scores(c, g):
                pe.wait_ge(onehot_ready, c + 1)
                pe.wait_ge(picked, count((c * TG + (g - 1 if g else 0)) * G))
                for j in range(G):
                    t = g * G + j
                    for k in range(3):
                        last = nc.tensor.matmul(ps_pick[:, g % 2, j * NPP:(j + 1) * NPP],
                                                onehot[:, t * P:(t + 1) * P], s_dst[:, k, :],
                                                start=(k == 0), stop=(k == 2))
                last.then_inc(pick_mm, 1)

            def attr_product(i, u):
                pe.wait_ge(attr_in[u], (i + 1) * 16)
                for b in range(2):
                    last = nc.tensor.matmul(ps_attr[0:G * F_EDGE, b, 0:TG * P // 2], attr_w[:],
                                            attr_sb[u][:, b * (TG * P // 2):(b + 1) * (TG * P // 2)],
                                            start=True, stop=True)
                last.then_inc(attr_mm, 1)

            def chunk(i, u, final):
                c = i * U + u
                dst_scores(c, 0)
                dst_scores(c, 1)
                if not final:
                    select(c + 1, 0)
                dst_scores(c, 2)
                dst_scores(c, 3)
                pe.wait_ge(eae_ready, count(c + 1))
                if not final:
                    attr_product(i if u < U - 1 else i + 1, (u + 1) % U)
                pe.wait_ge(msg_added, count(c))
                pe.wait_ge(signs_summed, count(c + 1))
                eae_flat = eae.rearrange("k a b -> k (a b)")
                for g in range(TG):
                    last = nc.tensor.matmul(ps_msg[:, g // 3, g % 3 * G * VW:(g % 3 + 1) * G * VW],
                                            eae_flat[:, g * P:(g + 1) * P], msg_w[:], start=True, stop=True)
                last.then_inc(msg_mm, 1)
                dst_scores(c, 4)
                if not final:
                    for j in range(1, TS):
                        select(c + 1, j)
                pe.wait_ge(signs_ready, c + 1)
                pe.wait_ge(msg_added, count(c + 1))
                for t in range(T):
                    last = nc.tensor.matmul(ps_signs, sign_hi[:, t, :], sign_lo[:, t, :], start=(t == 0),
                                            stop=(t == T - 1))
                last.then_inc(signs_mm, 1)

            attr_product(0, 0)
            pe.wait_ge(parts_ready, 1)
            for j in range(TS):
                select(0, j)
            with pe.Fori(0, ITERS - 1) as i:
                for u in range(U):
                    chunk(i, u, False)
            for u in range(U):
                chunk(ITERS - 1, u, u == U - 1)
            pe.wait_ge(sign_parts_ready, 1)
            for k in range(3):
                last = nc.tensor.matmul(ps_misc[:, 1, 0:NPP], differ[:], sign_parts[:, k, :], start=(k == 0),
                                        stop=(k == 2))
            last.then_inc(differ_mm, 1)
            flag = is_unsorted(pe)
            with pe.If(flag < 1):
                pe.wait_ge(tails_in, 16)
                pe.wait_ge(head_idx_ready, 1)
                nc.tensor.transpose(ps_misc[:, 0, 0:P], mtail[:], ident[:]).then_inc(mtail_mm, 1)
                pe.wait_ge(texp_done, 1)
                nc.tensor.transpose(ps_misc[:, 0, P:2 * P], wtail[:], ident[:]).then_inc(wtailT_mm, 1)
                pe.wait_ge(wtailT_sb, 1)
                nc.tensor.matmul(ps_misc[:, 0, 2 * P:2 * P + VW], wtailT[:], tails[:, 0:VW], start=True,
                                 stop=True).then_inc(tsum_mm, 1)
            with pe.If(flag >= 1):
                with pe.Fori(0, EPP) as t:
                    pe.wait_ge(merge_keys, t + 1)
                    nc.tensor.transpose(ps_misc[:, 0, 0:P], mtail[:], ident[:])
                    nc.tensor.transpose(ps_misc[:, 0, P:2 * P], contrib[:], ident[:]).then_inc(merge_keys_mm, 1)
                    pe.wait_ge(merge_exp, t + 1)
                    nc.tensor.transpose(ps_misc[:, 1, 0:P], wtail[:], ident[:]).then_inc(merge_wT_mm, 1)
                    pe.wait_ge(merge_wT_sb, t + 1)
                    nc.tensor.matmul(ps_misc[:, 1, 2 * P:2 * P + VW], wtailT[:], tile_rows[:, 0:VW], start=True,
                                     stop=True).then_inc(merge_sum_mm, 1)

        @block.vector
        def _(dve):
            v = nc.vector
            dve.sem_inc(tab_sb, 2)
            start_at_one(dve, maskT_sb, eae_ready, signs_summed, picked, msg_added, sums_ready, sel_read)
            steps = [0]

            def done(ins, at=0):
                steps[0] += 1
                ins.then_inc(dve_step, 1)
                dve.wait_ge(dve_step, at + steps[0])

            def stage(own_steps):
                taken = [0]

                def stage_done(ins, at=0):
                    taken[0] += 1
                    ins.then_inc(own_steps, 1)
                    dve.wait_ge(own_steps, at + taken[0])
                return stage_done

            v.memset(keep[:, :, 0:1], 0.0)
            v.memset(sums[:], 0.0).then_inc(zeros_ready, 1)
            v.memset(sign_sums[:], 0.0)
            v.memset(ps_signs, 0.0)
            done(v.memset(mrun[:], 0.0))
            dve.wait_ge(weights_in, 9 * 16)
            v.tensor_copy(het_bT7[:], het_bT[:].unsqueeze(1).broadcast_to([F_IN, N7, N_NODE_TYPES])).then_inc(
                node_b7_ready, 1)
            dve.wait_ge(x_in, 32)
            sq = table[:, :, 0:F_IN]
            done(v.tensor_reduce(stat[:, 0, :], x_sb, AX.X, ALU.add))
            done(v.tensor_scalar(stat[:, 1, :], stat[:, 0, :], 1.0 / F_IN, None, ALU.mult))
            done(v.tensor_tensor(h[:], x_sb, stat[:, 1, :].unsqueeze(2).broadcast_to([P, NPP, F_IN]), ALU.subtract))
            done(v.tensor_tensor(sq, h[:], h[:], ALU.mult))
            done(v.tensor_reduce(stat[:, 0, :], sq, AX.X, ALU.add))
            v.tensor_scalar(stat[:, 2, :], stat[:, 0, :], 1.0 / F_IN, 1e-5, ALU.mult, ALU.add).then_inc(var_ready, 1)
            done(v.tensor_copy(ntype_f[:], ntype[:]))
            dve.wait_ge(consts, 9)
            done(v.tensor_tensor(tmask[:], ntype_f[:].unsqueeze(2).broadcast_to([P, NPP, N_NODE_TYPES]),
                                 types8[:, 0:N_NODE_TYPES].unsqueeze(1).broadcast_to([P, NPP, N_NODE_TYPES]),
                                 ALU.is_equal))
            dve.wait_ge(dev_ready, 1)
            done(v.reciprocal(stat[:, 0, :], stat[:, 3, :]))
            done(v.scalar_tensor_tensor(h[:], h[:], 0.0, stat[:, 0, :].unsqueeze(2).broadcast_to([P, NPP, F_IN]),
                                        ALU.max, ALU.mult))
            done(v.tensor_scalar(group_sel[:], group_row[:], 0.0, None, ALU.is_ge))
            done(v.scalar_tensor_tensor(group_sel[:], group_row[:], float(N_NODE_TYPES - 1), group_sel[:], ALU.is_le,
                                        ALU.mult))
            dve.wait_ge(node_w_sb, 1)
            v.tensor_tensor(node_b7[:], node_b[:].unsqueeze(1).broadcast_to([MB, N7, YW]),
                            group_sel[:].unsqueeze(2).broadcast_to([MB, N7, YW]), ALU.mult).then_inc(node_b7_ready, 1)

            def by_type(n, k):
                v.tensor_tensor(hm[k][:].rearrange("p n (k f) -> p n k f", f=F_IN),
                                h[:, ds(n * N7, N7), :].unsqueeze(2).broadcast_to([P, N7, N_NODE_TYPES, F_IN]),
                                tmask[:, ds(n * N7, N7), :].unsqueeze(3).broadcast_to([P, N7, N_NODE_TYPES, F_IN]),
                                ALU.mult)
                v.tensor_copy(hmask[k][:].rearrange("p (n k) -> p n k", k=N_NODE_TYPES),
                              tmask[:, ds(n * N7, N7), :]).then_inc(hm_ready, 1)

            def from_psum(n, k):
                dve.wait_ge(hmT_mm, n + 1)
                dve.wait_ge(tab_mm, n + 1)
                v.tensor_copy(maskT[k][:], ps_msg[0:MB, k, 0:P]).then_inc(maskT_sb, 1)

            def table_rows(n, k):
                dve.wait_ge(tab_mm, n + 3)
                v.tensor_scalar(table[:, ds(n * N7, N7), :],
                                ps_misc[:, k, 0:N7 * YW].rearrange("p (n f) -> p n f", f=YW), 1.0, None,
                                ALU.mult).then_inc(tab_sb, 1)

            by_type(0, 0)
            by_type(1, 1)
            with dve.Fori(0, NODE_ITERS // 2 - 1) as i:
                from_psum(i * 2, 0)
                from_psum(i * 2 + 1, 1)
                by_type(i * 2 + 2, 0)
                table_rows(i * 2, 0)
                by_type(i * 2 + 3, 1)
                table_rows(i * 2 + 1, 1)
            from_psum(NODE_ITERS - 2, 0)
            from_psum(NODE_ITERS - 1, 1)
            table_rows(NODE_ITERS - 2, 0)
            table_rows(NODE_ITERS - 1, 1)
            dve.wait_ge(tab_sb, NODE_ITERS + 2)
            score = table[:, :, F_IN + 1]
            done(v.tensor_copy(s_dst[:, 0, :], score))
            done(v.tensor_tensor(s_rest[:], score, s_dst[:, 0, :], ALU.subtract))
            done(v.tensor_copy(s_dst[:, 1, :], s_rest[:]))
            done(v.tensor_tensor(s_rest[:], s_rest[:], s_dst[:, 1, :], ALU.subtract))
            v.tensor_copy(s_dst[:, 2, :], s_rest[:]).then_inc(s_parts, 1)

            def div98(to, src, at=0):
                done(v.tensor_scalar(to, src, 1.0 / NPP, 0.5 / NPP - 0.5, ALU.mult, ALU.add), at)
                done(v.tensor_scalar(to, to, ROUND, ROUND, ALU.add, ALU.subtract), at)

            dve.wait_ge(dst_in, 16)
            done(v.tensor_copy(dst_f[:], dst_i))
            div98(hi_f[:], dst_f[:])
            v.tensor_copy(hi_b, hi_f[:]).then_inc(hi_ready, 1)
            dve.wait_ge(sel_in, 16)
            node, row, group = sel_tmp[1:4]
            done(v.tensor_copy(node, sel_tmp[0].bitcast(i32)))
            div98(row, node)
            done(v.scalar_tensor_tensor(node, row, -float(NPP), node, ALU.mult, ALU.add))
            done(v.tensor_scalar(group, node, 1.0 / GN, 0.5 / GN - 0.5, ALU.mult, ALU.add))
            done(v.tensor_scalar(group, group, ROUND, ROUND, ALU.add, ALU.subtract))
            v.scalar_tensor_tensor(sel_code[:], group[:, 0:SEL], float(P), row[:, 0:SEL], ALU.mult,
                                   ALU.add).then_inc(codes_ready, 1)
            done(v.scalar_tensor_tensor(sel_node[:], group[:, SEL:2 * SEL], -float(GN), node[:, SEL:2 * SEL], ALU.mult,
                                        ALU.add))
            done(v.scalar_tensor_tensor(emb_act[:], emb[:], SLOPE, emb[:], ALU.mult, ALU.max))
            done(v.tensor_tensor(emb_act[:], emb_act[:], att_type[:].unsqueeze(1).broadcast_to(
                [P, N_EDGE_TYPES, F_EDGE]), ALU.mult))
            done(v.tensor_reduce(type_score[:], emb_act[:], AX.X, ALU.add))

            v.tensor_scalar(half128[:], free128[:], 0.5, None, ALU.add)
            done(v.tensor_scalar(wtail[:], free128[:], part[:, 0:1], None, ALU.subtract))
            v.tensor_scalar(mtail[:], wtail[:], 1.0, None, ALU.is_equal)
            done(v.tensor_scalar(wtailT[:], wtail[:], -(P - 1.0), None, ALU.is_equal))
            done(v.tensor_tensor(mtail[:], wtailT[:], mtail[:], ALU.subtract))
            v.tensor_tensor(differ[:], ident[:], mtail[:], ALU.add)
            done(v.tensor_copy(redge[:], redge_i[:]))
            done(v.tensor_copy(rlast[:], rlast_i[:]))
            dve.wait_ge(dst_in, 32)
            done(v.tensor_copy(dst_f[:], dst_i))
            v.memset(before_me[:], 1.0)
            done(v.scalar_tensor_tensor(hi_f[:, 0:EPP - 1], dst_f[:, 0:EPP - 1], 1.0, dst_f[:, 1:EPP], ALU.mult,
                                        ALU.is_gt, accum_out=falls[:, 0:1]))
            done(v.tensor_tensor(falls[:, 1:2], redge[:, 2:3], redge[:, 0:1], ALU.is_gt))
            v.tensor_tensor(falls[:, 0:1], falls[:, 0:1], falls[:, 1:2], ALU.add).then_inc(falls_ready, 1)
            dve.wait_ge(falls_mm, 1)
            done(v.tensor_scalar(unsorted[:], ps_misc[:, 0, 0:1], 1.0, None, ALU.min))
            v.tensor_copy(unsorted_i[:], unsorted[:]).then_inc(unsorted_ready, 1)
            v.tensor_scalar(dst_f[:], dst_f[:], redge[:, 0:1], 0.0, ALU.is_equal, ALU.add,
                            accum_out=head[:, 0:1]).then_inc(head_counted, 1)
            dve.wait_ge(head_counted, 1)
            done(v.scalar_tensor_tensor(head[:, 1:2], part[:], float(EPP), head[:, 0:1], ALU.mult, ALU.add))
            done(v.tensor_scalar(head[:, 1:2], head[:, 1:2], -1.0, None, ALU.add))
            done(v.tensor_tensor(head[:, 2:3], redge[:, 0:1], redge[:, 2:3], ALU.is_equal))
            done(v.tensor_tensor(head[:, 3:4], redge[:, 1:2], redge[:, 3:4], ALU.is_equal))
            done(v.scalar_tensor_tensor(head[:, 3:4], head[:, 0:1], float(EPP), head[:, 3:4], ALU.is_equal, ALU.mult))
            done(v.scalar_tensor_tensor(head[:, 4:5], head[:, 3:4], 0.0, head[:, 2:3], ALU.is_equal, ALU.mult))
            done(v.tensor_scalar(head[:, 5:6], head[:, 4:5], -float(2 ** 21), float(2 ** 21), ALU.mult, ALU.add))
            done(v.tensor_tensor(head[:, 5:6], head[:, 5:6], head[:, 1:2], ALU.add))
            done(v.tensor_copy(head_idx[:, 0:1], head[:, 1:2]))
            done(v.tensor_copy(head_idx[:, 1:2], head[:, 5:6]))
            done(v.tensor_scalar(contrib[:], free128[:], part[:, 0:1], None, ALU.is_lt))
            done(v.scalar_tensor_tensor(contrib[:], rlast[:], redge[:, 0:1], contrib[:], ALU.is_equal, ALU.mult))
            rest = rows[0][:].rearrange("p a b -> p (a b)")[:, 0:VW * GN].rearrange("p (f n) -> p f n", n=GN)
            for g in range(NG):
                whole = table[:, g * GN:(g + 1) * GN, 0:VW].rearrange("p n f -> p f n")
                part_of = [parts[:, k, g, :].rearrange("p (f n) -> p f n", n=GN) for k in range(3)]
                done(v.tensor_copy(part_of[0], whole))
                done(v.tensor_tensor(rest, whole, part_of[0], ALU.subtract))
                done(v.tensor_copy(part_of[1], rest))
                done(v.tensor_tensor(rest, rest, part_of[1], ALU.subtract))
                last = v.tensor_copy(part_of[2], rest)
                if g < NG - 1:
                    done(last)
            last.then_inc(parts_ready, 1)
            dve.wait_ge(parts_ready, 1)
            dve.wait_ge(table_out, 16)
            v.memset(last_rows[:, :, 0:VW], 0.0)
            v.memset(last_rows[:, :, VW:VW + 1], -BIG)
            v.memset(last_rows[:, :, VW + 1:RW], -1.0).then_inc(node_rows_ready, 1)


            def select_onehots(u, tiles, ready):
                for g in range(NG):
                    last = v.tensor_scalar(sel_onehot[:, g, tiles], code_sb[u][:, tiles], part_group[:, g:g + 1],
                                           None, ALU.is_equal)
                last.then_inc(ready, 1)

            def select_first(i, u):
                c = i * U + u
                dve.wait_ge(code_in[u], (i + 1) * 16)
                if not isinstance(c, int) or c:
                    dve.wait_ge(sel_mm, count(c * TS - TS + 1))
                select_onehots(u, slice(0, P), sel_first_ready)

            def select_others(i, u, at=0):
                c = i * U + u
                dve.wait_ge(sel_mm, count(c * TS))
                select_onehots(u, slice(P, TS * P), sel_onehot_ready)
                done(v.tensor_tensor(sel_mask[:], sel_node[:, ds(c * TS, TS)].unsqueeze(2).broadcast_to([P, TS, GN]),
                                     free98[:, 0:GN].unsqueeze(1).broadcast_to([P, TS, GN]), ALU.is_equal), at)

            def take(c, u, j, at=0):
                dve.wait_ge(sel_mm, count(c * TS + j + 1))
                v.tensor_tensor(sel_prod, ps_sel[:, j % 2, 0:VW * GN].rearrange("p (f n) -> p f n", n=GN),
                                sel_mask[:, j:j + 1, :].broadcast_to([P, VW, GN]), ALU.mult).then_inc(sel_read, 1)
                dve.wait_ge(sel_read, count(c * TS + j + 1))
                done(v.tensor_reduce(gath[u][:, TD + j, 0:VW], sel_prod, AX.X, ALU.add), at)

            def picks(c, u, g):
                dve.wait_ge(pick_mm, count(c * TG + g + 1))
                for j in range(G):
                    t = g * G + j
                    v.scalar_tensor_tensor(pick[:, t, :], free98[:], loc[u][:, t:t + 1],
                                           ps_pick[:, g % 2, j * NPP:(j + 1) * NPP], ALU.is_equal, ALU.mult,
                                           accum_out=dscore[:, t:t + 1]).then_inc(picked, 1)

            def places(i, u, at=0):
                dve.wait_ge(meta_in[u], (i + 1) * 16)
                done(v.tensor_copy(dstc[u][:], meta_sb[u][:, T:2 * T + 1]), at)
                div98(hic[u][:], dstc[u][:, 1:T + 1], at)
                v.scalar_tensor_tensor(loc[u][:], hic[u][:], -float(NPP), dstc[u][:, 1:T + 1], ALU.mult,
                                       ALU.add).then_inc(places_ready, 1)

            def sum_signs(c):
                dve.wait_ge(signs_mm, count(c))
                dve.wait_ge(signs_summed, count(c))
                v.tensor_tensor(sign_sums[:], sign_sums[:], ps_signs, ALU.add).then_inc(signs_summed, 1)

            def dst_onehot(i, u):
                dve.wait_ge(hib_in[u], (i + 1) * 16)
                v.tensor_scalar(onehot[:], hib_sb[u][:], part[:, 0:1], None, ALU.is_equal).then_inc(
                    onehot_ready, 1)

            def chunk(i, u, at, final):
                c = i * U + u
                after = (i if u < U - 1 else i + 1, (u + 1) % U)
                m = meta_sb[u]
                dve.wait_ge(places_ready, c + 1)
                picks(c, u, 0)
                picks(c, u, 1)
                sum_signs(c)
                dve.wait_ge(eae_scaled, c + 1)
                dve.wait_ge(msg_mm, count(c))
                v.tensor_tensor(eae, eae_s, ps_attr[0:G * F_EDGE, :, 0:TG * P // 2], ALU.max).then_inc(
                    eae_ready, 1)
                if not final:
                    select_others(*after, at)
                    take(c + 1, (u + 1) % U, 0, at)
                    if not isinstance(i, int) or c + 2 < CHUNKS:
                        select_first(i if u < U - 2 else i + 1, (u + 2) % U)
                picks(c, u, 2)
                picks(c, u, 3)
                picks(c, u, 4)
                if not final:
                    dst_onehot(*after)
                done(v.tensor_tensor(pen[:], dstc[u][:, 1:T + 1], dstc[u][:, 0:T], ALU.is_equal), at)
                done(v.tensor_scalar(pen[:], pen[:], BIG, BIG, ALU.mult, ALU.subtract), at)
                done(v.tensor_copy(etc[:], m[:, 2 * T + 1:3 * T + 1]), at)
                done(v.tensor_tensor(emask[:], etc[:].unsqueeze(2).broadcast_to([P, T, N_EDGE_TYPES]),
                                     types8[:].unsqueeze(1).broadcast_to([P, T, N_EDGE_TYPES]), ALU.is_equal), at)
                done(v.tensor_tensor(emask[:], emask[:], type_score[:].unsqueeze(1).broadcast_to(
                    [P, T, N_EDGE_TYPES]), ALU.mult), at)
                done(v.tensor_reduce(escore[:], emask[:], AX.X, ALU.add), at)
                dve.wait_ge(picked, count((c + 1) * T))
                done(v.tensor_tensor(escore[:], escore[:], dscore[:], ALU.add), at)
                dve.wait_ge(gathered[u], (i + 1) * (16 * TD))
                dve.wait_ge(msg_mm, count(c + 1))
                v.tensor_tensor(msg[:, 0:3 * G, :], gath[u][:, 0:3 * G, 0:VW],
                                ps_msg[:, 0, 0:3 * G * VW].rearrange("p (t f) -> p t f", f=VW), ALU.add)
                v.tensor_tensor(msg[:, 3 * G:T, :], gath[u][:, 3 * G:T, 0:VW],
                                ps_msg[:, 1, 0:2 * G * VW].rearrange("p (t f) -> p t f", f=VW),
                                ALU.add).then_inc(msg_added, 1)
                dve.wait_ge(msg_added, count(c + 1))
                done(v.tensor_tensor(alpha[:], msg[:, :, F_IN], escore[:], ALU.add), at)
                done(v.scalar_tensor_tensor(alpha[:], alpha[:], SLOPE, alpha[:], ALU.mult, ALU.max), at)
                done(v.tensor_copy(mrun[:, 0:1], mrun[:, T:T + 1]), at)
                done(v.tensor_tensor_scan(mrun[:, 1:T + 1], pen[:], alpha[:], mrun[:, 0:1], ALU.add, ALU.max), at)
                v.tensor_tensor(args[:, 0, :], alpha[:], mrun[:, 1:T + 1], ALU.subtract)
                done(v.tensor_tensor(args[:, 1, :], mrun[:, 0:T], pen[:], ALU.add), at)
                v.tensor_tensor(args[:, 1, :], args[:, 1, :], mrun[:, 1:T + 1], ALU.subtract).then_inc(
                    args_ready, 1)
                v.tensor_copy(terms[:, :, 0:1], sums[:, :, T:T + 1])
                if not final:
                    take(c + 1, (u + 1) % U, 1, at)
                dve.wait_ge(exp_done, c + 1)
                v.tensor_copy(terms[:, F_IN, 1:T + 1], wts[:, 0, :])
                done(v.tensor_tensor(terms[:, 0:F_IN, 1:T + 1].rearrange("p f t -> p t f"), msg[:, :, 0:F_IN],
                                     wts[:, 0, :].unsqueeze(2).broadcast_to([P, T, F_IN]), ALU.mult), at)
                dve.wait_ge(keep_ready, c + 1)
                dve.wait_ge(rows_sums, count(c))
                v.tensor_tensor_scan(sums[:].rearrange("p f t -> p (f t)"), keep[:].rearrange("p f t -> p (f t)"),
                                     terms.rearrange("p f t -> p (f t)"), 0.0, ALU.mult,
                                     ALU.add).then_inc(sums_ready, 1)
                dve.wait_ge(sums_ready, count(c + 1))
                if not final:
                    places(*after, at)
                    for j in range(2, TS):
                        take(c + 1, (u + 1) % U, j, at)

            dve.wait_ge(node_rows_out, 16)
            places(0, 0)
            select_first(0, 0)
            select_others(0, 0)
            dst_onehot(0, 0)
            for j in range(TS):
                take(0, 0, j)
            select_first(0, 1)
            before = steps[0]
            STEPS = 17 + TS
            with dve.Fori(0, ITERS - 1) as i:
                for u in range(U):
                    chunk(i, u, i * (U * STEPS), False)
            assert steps[0] == before + U * STEPS
            steps[0] = before + U * STEPS * (ITERS - 1)
            for u in range(U):
                chunk(ITERS - 1, u, 0, u == U - 1)

            sum_signs(CHUNKS)
            dve.wait_ge(signs_summed, count(CHUNKS + 1))
            done(v.tensor_copy(sign_parts[:, 0, :], sign_sums[:]))
            done(v.tensor_tensor(cnt[:], sign_sums[:], sign_parts[:, 0, :], ALU.subtract))
            done(v.tensor_copy(sign_parts[:, 1, :], cnt[:]))
            done(v.tensor_tensor(cnt[:], cnt[:], sign_parts[:, 1, :], ALU.subtract))
            v.tensor_copy(sign_parts[:, 2, :], cnt[:]).then_inc(sign_parts_ready, 1)
            dve.wait_ge(differ_mm, 1)
            done(v.tensor_scalar(fix[:, 0:1], ps_misc[:, 1, NPP - 1:NPP], -0.25, N_EDGES / 2 - 1.0, ALU.mult,
                                 ALU.add))
            done(v.scalar_tensor_tensor(fix[:, 0:1], sign_sums[:, NPP - 1:NPP], 0.5, fix[:, 0:1], ALU.mult, ALU.add))
            done(v.tensor_scalar(cnt[:], ps_misc[:, 1, 0:NPP], 0.25, fix[:, 0:1], ALU.mult, ALU.add))
            done(v.tensor_scalar(cnt[:], cnt[:], 0.0, None, ALU.max))
            done(v.tensor_scalar(scale[:, 0, :], node_id[:, 0:NPP], float(N_EDGES), None, ALU.add))
            done(v.tensor_tensor(scale[:, 0, :], scale[:, 0, :], cnt[:], ALU.subtract))
            done(v.scalar_tensor_tensor(cnt[:], scale[:, 0, :], unsorted[:, 0:1], cnt[:], ALU.mult, ALU.add))
            v.tensor_copy(pos[:], cnt[:]).then_inc(pos_ready, 1)

            flag = is_unsorted(dve)
            with dve.If(flag < 1):
                joined_step = stage(join_step)
                dve.wait_ge(tails_in, 16)
                v.tensor_copy(mtail[:], tails[:, VW:VW + 1].broadcast_to([P, P])).then_inc(head_idx_ready, 1)
                dve.wait_ge(mtail_mm, 1)
                joined_step(v.tensor_tensor(mtail[:], ps_misc[:, 0, 0:P], contrib[:], ALU.mult))
                joined_step(v.tensor_scalar(wtailT[:], contrib[:], BIG, BIG, ALU.mult, ALU.subtract))
                joined_step(v.tensor_tensor(mtail[:], mtail[:], wtailT[:], ALU.add))
                joined_step(v.tensor_reduce(fix[:, 0:1], mtail[:], AX.X, ALU.max))
                dve.wait_ge(own_in, 16)
                joined_step(v.tensor_tensor(fix[:, 0:1], fix[:, 0:1], own[:, VW:VW + 1], ALU.max))
                joined_step(v.tensor_tensor(fix[:, 1:2], own[:, VW:VW + 1], fix[:, 0:1], ALU.subtract))
                v.tensor_scalar(mtail[:], mtail[:], fix[:, 0:1], None, ALU.subtract).then_inc(targs_ready, 1)
                dve.wait_ge(wtailT_mm, 1)
                v.tensor_copy(wtailT[:], ps_misc[:, 0, P:2 * P]).then_inc(wtailT_sb, 1)
                v.tensor_copy(joined[:, VW:VW + 1], fix[:, 0:1])
                v.tensor_copy(joined[:, VW + 1:RW], own[:, VW + 1:RW])
                dve.wait_ge(tsum_mm, 1)
                v.scalar_tensor_tensor(joined[:, 0:VW], own[:, 0:VW], fix[:, 2:3], ps_misc[:, 0, 2 * P:2 * P + VW],
                                       ALU.mult, ALU.add).then_inc(joined_ready, 1)
            with dve.If(flag >= 1):
                merged_step = stage(merge_step)
                merged_step(v.tensor_scalar(before_me[:], free128[:], part[:, 0:1], None, ALU.is_gt))
                merged_step(v.memset(mg[:], 0.0))
                STEPS = 14
                with dve.Fori(0, EPP) as t:
                    at = t * STEPS
                    dve.wait_ge(tile_in, t * 32 + 32)
                    merged_step(v.tensor_scalar(mg[:, 0:1], mg[:, 0:1], 1.0, None, ALU.add), at)
                    merged_step(v.tensor_scalar(mg[:, 1:2], mg[:, 0:1], float(EPP), None, ALU.is_equal), at)
                    merged_step(v.tensor_tensor(mg[:, 2:3], tile_rows[:, VW + 1:RW], next_row[:, 1:2], ALU.not_equal), at)
                    merged_step(v.tensor_tensor(mg[:, 1:2], mg[:, 1:2], mg[:, 2:3], ALU.max), at)
                    merged_step(v.tensor_scalar(mg[:, 3:4], tile_rows[:, VW + 1:RW], part[:, 0:1], 1.0, ALU.add,
                                                ALU.add), at)
                    merged_step(v.scalar_tensor_tensor(mg[:, 3:4], mg[:, 3:4], mg[:, 1:2], part[:], ALU.mult,
                                                       ALU.subtract), at)
                    merged_step(v.tensor_scalar(mg[:, 3:4], mg[:, 3:4], -1.0, None, ALU.add), at)
                    v.tensor_copy(mtail[:], mg[:, 3:4].broadcast_to([P, P]))
                    v.tensor_copy(contrib[:], tile_rows[:, VW:VW + 1].broadcast_to([P, P])).then_inc(merge_keys, 1)
                    v.tensor_scalar(merge_idx[:, 0:1], tile_rows[:, VW + 1:RW], float(N_EDGES), None,
                                    ALU.add).then_inc(merge_idx_ready, 1)
                    dve.wait_ge(merge_keys_mm, t + 1)
                    merged_step(v.tensor_scalar(wtailT[:], ps_misc[:, 0, 0:P], mg[:, 3:4], None, ALU.is_equal), at)
                    merged_step(v.tensor_tensor(mtail[:], wtailT[:], ps_misc[:, 0, P:2 * P], ALU.mult), at)
                    v.tensor_tensor(contrib[:], wtailT[:], before_me[:], ALU.mult)
                    merged_step(v.tensor_scalar(wtailT[:], wtailT[:], BIG, BIG, ALU.mult, ALU.subtract), at)
                    v.tensor_tensor(mtail[:], mtail[:], wtailT[:], ALU.add)
                    merged_step(v.tensor_reduce(mg[:, 5:6], contrib[:], AX.X, ALU.add), at)
                    v.scalar_tensor_tensor(mg[:, 5:6], mg[:, 5:6], 0.0, mg[:, 1:2], ALU.is_equal, ALU.mult)
                    merged_step(v.tensor_reduce(fix[:, 0:1], mtail[:], AX.X, ALU.max), at)
                    merged_step(v.tensor_scalar(mg[:, 5:6], mg[:, 5:6], -float(2 ** 21), float(2 ** 21) + N_EDGES,
                                                ALU.mult, ALU.add), at)
                    dve.wait_ge(node_in, t * 16 + 16)
                    v.tensor_tensor(merge_idx[:, 1:2], mg[:, 5:6], tile_rows[:, VW + 1:RW], ALU.add)
                    merged_step(v.tensor_tensor(fix[:, 0:1], fix[:, 0:1], own[:, VW:VW + 1], ALU.max), at)
                    v.tensor_tensor(fix[:, 1:2], own[:, VW:VW + 1], fix[:, 0:1], ALU.subtract)
                    v.tensor_scalar(mtail[:], mtail[:], fix[:, 0:1], None, ALU.subtract).then_inc(merge_args, 1)
                    dve.wait_ge(merge_wT_mm, t + 1)
                    v.tensor_copy(wtailT[:], ps_misc[:, 1, 0:P]).then_inc(merge_wT_sb, 1)
                    v.tensor_copy(joined[:, VW:VW + 1], fix[:, 0:1])
                    v.tensor_copy(joined[:, VW + 1:RW], tile_rows[:, VW + 1:RW])
                    dve.wait_ge(merge_sum_mm, t + 1)
                    v.scalar_tensor_tensor(joined[:, 0:VW], own[:, 0:VW], fix[:, 2:3],
                                           ps_misc[:, 1, 2 * P:2 * P + VW], ALU.mult,
                                           ALU.add).then_inc(merge_row_ready, 1)
            finished = stage(last_step)
            dve.wait_ge(last_in, 16 * NPP)
            dve.wait_ge(x_in, 48)
            finished(v.tensor_tensor(scale[:, 0, :], last_rows[:, :, VW + 1], node_id[:, 0:NPP], ALU.is_equal))
            finished(v.tensor_scalar(scale[:, 1, :], last_rows[:, :, F_IN], 1e-16, None, ALU.add))
            finished(v.reciprocal(scale[:, 1, :], scale[:, 1, :]))
            finished(v.tensor_tensor(scale[:, 0, :], scale[:, 0, :], scale[:, 1, :], ALU.mult))
            finished(v.tensor_tensor(h[:], last_rows[:, :, 0:F_IN], scale[:, 0, :].unsqueeze(2).broadcast_to(
                [P, NPP, F_IN]), ALU.mult))
            v.tensor_tensor(h[:], h[:], x_sb, ALU.add).then_inc(out_ready, 1)


def kernel(x, src, dst, edge_attr_16, edge_type_8, node_type_4, L0_gnn_hetero_w, L0_gnn_hetero_b,
           L0_gnn_edge_type_emb, L0_gnn_edge_attr_w, L0_gnn_att_w, L0_gnn_lin_w):
    import numpy as np
    import concourse.bacc as bacc
    from concourse.bass_utils import run_bass_kernel_spmd

    x, src, dst = np.asarray(x), np.asarray(src), np.asarray(dst)
    node_type, edge_type = np.asarray(node_type_4), np.asarray(edge_type_8)
    pad = N_PAD - N_NODES
    rows = dst.reshape(P, EPP)
    before = np.full((P, 1), -1, dst.dtype)
    dst_prev = np.concatenate([before, rows], axis=1)
    windows = np.stack([dst_prev[:, c * T:(c + 1) * T + 1] for c in range(CHUNKS)], axis=1)
    meta = np.concatenate([src.reshape(P, CHUNKS, T), windows, edge_type.reshape(P, CHUNKS, T)], axis=2)
    none = np.full((1,), -1, dst.dtype)
    row_edges = np.stack([rows[:, 0], rows[:, -1], np.concatenate([none, rows[:-1, -1]]),
                          np.concatenate([rows[1:, 0], none])], axis=1)
    attr = np.asarray(edge_attr_16).reshape(P, CHUNKS, TG, G, F_EDGE).transpose(3, 4, 1, 2, 0)
    sel = src.reshape(P, CHUNKS, T)[:, :, TD:]
    arrays = {
        "x_in": np.concatenate([x, np.zeros((pad, F_IN), x.dtype)]).reshape(P, NPP, F_IN),
        "meta_in": meta,
        "dst_rows_in": rows,
        "dst_tmajor_in": rows.T.reshape(P, EPP),
        "sel_src_in": np.concatenate([sel.transpose(1, 2, 0).reshape(P, SEL), sel.reshape(P, SEL)], axis=1),
        "row_edges_in": row_edges,
        "row_last_in": rows[:, -1],
        "edge_attr_t_in": attr.reshape(G * F_EDGE, CHUNKS, TG * P),
        "node_type_in": np.concatenate([node_type, np.zeros((pad,), node_type.dtype)]).reshape(P, NPP),
        "hetero_wT_in": np.asarray(L0_gnn_hetero_w).transpose(2, 0, 1).reshape(F_IN, N_NODE_TYPES * F_IN),
        "hetero_bT_in": np.asarray(L0_gnn_hetero_b).T,
        "edge_type_emb_in": np.asarray(L0_gnn_edge_type_emb),
        "edge_attr_w_in": np.asarray(L0_gnn_edge_attr_w),
        "att_w_in": np.asarray(L0_gnn_att_w),
        "lin_w_in": np.asarray(L0_gnn_lin_w),
    }
    nc = bacc.Bacc("TRN2", target_bir_lowering=False, num_devices=1)
    args = []
    for name in list(arrays):
        arrays[name] = np.ascontiguousarray(arrays[name])
        args.append(nc.dram_tensor(name, arrays[name].shape, mybir.dt.from_np(arrays[name].dtype),
                                   kind="ExternalInput").ap())
    out = nc.dram_tensor("out_dram", (P, NPP, F_IN), mybir.dt.float32, kind="ExternalOutput").ap()
    gnn_kernel(nc, *args, out)
    result = run_bass_kernel_spmd(nc, [arrays], core_ids=[0])
    return result.results[0]["out_dram"].reshape(N_PAD, F_IN)[:N_NODES]
```

```python
import concourse.bass as bass
from concourse import mybir
from contextlib import ExitStack

N_NODES = 12500
N_EDGES = 400000
F_IN = 32
F_EDGE = 16
N_NODE_TYPES = 4
N_EDGE_TYPES = 8
SLOPE = 0.2

P = 128
EPP = N_EDGES // P
NPP = -(-N_NODES // P)
N_PAD = P * NPP
T = 25
CHUNKS = EPP // T
U = 5
ITERS = CHUNKS // U
TS = (4, 3, 4, 3, 4)
TS_BEFORE = tuple(sum(TS[:u]) for u in range(U))
TS_ITER = sum(TS)
TSM = max(TS)
SEL = CHUNKS * TSM
G = 5
TG = T // G
YW = F_IN + 2
NG = 7
GN = NPP // NG
VW = F_IN + 1
RW = F_IN + 3
META = 3 * T + 1
BIG = 3.0e38
ROUND = 12582912.0
N7 = 7
NODE_ITERS = NPP // N7
WARM_UP = 14
PIECE = 80
MB = N7 * N_NODE_TYPES


def gnn_kernel(nc, x, meta, dst_rows, dst_tmajor, sel_src, row_edges, row_last, edge_attr_t, node_type,
               hetero_wT, hetero_bT, edge_type_emb, edge_attr_w, att_w, lin_w, out):
    fp32, bf16, i32 = mybir.dt.float32, mybir.dt.bfloat16, mybir.dt.int32
    ALU, ACT, AX = mybir.AluOpType, mybir.ActivationFunctionType, mybir.AxisListType
    ds = bass.ds

    table_dram = nc.dram_tensor("table_dram", (N_PAD, YW), fp32, kind="Internal").ap()
    dst_hi_dram = nc.dram_tensor("dst_hi_dram", (CHUNKS, T * P), bf16, kind="Internal").ap()
    sel_code_dram = nc.dram_tensor("sel_code_dram", (CHUNKS, TSM * P), mybir.dt.float16, kind="Internal").ap()
    rows_dram = nc.dram_tensor("rows_dram", (N_EDGES + N_PAD, RW), fp32, kind="Internal").ap()
    rows_pm = rows_dram[0:N_EDGES, :].rearrange("(p e) f -> p e f", p=P)
    rows_after = rows_dram[1:N_EDGES + 1, :].rearrange("(p e) f -> p e f", p=P)
    node_rows = rows_dram[N_EDGES:N_EDGES + N_PAD, :].rearrange("(p n) f -> p n f", p=P)

    ctx = ExitStack()
    with ctx:
        def sb(name, shape, dt=fp32):
            return ctx.enter_context(nc.sbuf_tensor(name, shape, dt))

        def sem(name):
            return ctx.enter_context(nc.semaphore(name))

        ident = sb("ident", [P, P])
        part = sb("part", [P, 1])
        free98 = sb("free98", [P, NPP])
        free128 = sb("free128", [P, P])
        half128 = sb("half128", [P, P])
        node_id = sb("node_id", [P, NPP])
        part_group = sb("part_group", [P, NG])
        group_row = sb("group_row", [MB, N7])
        group_sel = sb("group_sel", [MB, N7])
        types8 = sb("types8", [P, N_EDGE_TYPES])
        scores_w = sb("scores_w", [F_IN, YW])
        het_wT = sb("het_wT", [F_IN, P])
        het_bT = sb("het_bT", [F_IN, N_NODE_TYPES])
        node_w = sb("node_w", [P, YW])
        het_bT7 = sb("het_bT7", [F_IN, N7, N_NODE_TYPES])
        node_b = sb("node_b", [MB, YW])
        node_b7 = sb("node_b7", [MB, N7, YW])
        attr_w = sb("attr_w", [G * F_EDGE, G * F_EDGE])
        msg_w = sb("msg_w", [G * F_EDGE, G * VW])
        emb = sb("emb", [P, N_EDGE_TYPES, F_EDGE])
        emb_act = sb("emb_act", [P, N_EDGE_TYPES, F_EDGE])
        att_type = sb("att_type", [P, F_EDGE])
        type_score = sb("type_score", [P, N_EDGE_TYPES])

        parts = sb("parts", [P, 3, NG, VW * GN], bf16)
        x_sb = parts[:].rearrange("p k g m -> p (k g m)").bitcast(fp32)[:, 0:NPP * F_IN].rearrange(
            "p (n f) -> p n f", f=F_IN)
        h = sb("h", [P, NPP, F_IN])
        node_buf = sb("node_buf", [P, NPP * RW])
        table = node_buf[:, 0:NPP * YW].rearrange("p (n f) -> p n f", f=YW)
        last_rows = node_buf[:].rearrange("p (n f) -> p n f", f=RW)

        def in_node_buf(at, shape, parts=P):
            size = shape[0] * shape[1]
            return node_buf[0:parts, at:at + size].rearrange("p (a b) -> p a b", b=shape[1])
        stat = sb("stat", [P, 4, NPP])
        ntype = sb("ntype", [P, NPP], i32)
        ntype_f = sb("ntype_f", [P, NPP])
        tmask = sb("tmask", [P, NPP, N_NODE_TYPES])
        hm = [sb(f"hm{k}", [P, N7, P]) for k in range(2)]
        hmask = [sb(f"hmask{k}", [P, MB]) for k in range(2)]
        hmT = [sb(f"hmT{k}", [P, N7 * P]) for k in range(2)]
        maskT = [sb(f"maskT{k}", [MB, P]) for k in range(2)]
        s_rest = sb("s_rest", [P, NPP])
        s_dst = sb("s_dst", [P, 3, NPP], bf16)

        dst_f = sb("dst_f", [P, EPP])
        hi_f = sb("hi_f", [P, EPP])
        dst_i = hi_f[:].bitcast(i32)
        meta_sb = [sb(f"meta{u}", [P, META], i32) for u in range(U)]
        attr_sb = [sb(f"attr{u}", [G * F_EDGE, TG * P]) for u in range(U)]
        hib_sb = [sb(f"hib{u}", [P, T * P], bf16) for u in range(U)]
        gath = [sb(f"gath{u}", [P, T, YW]) for u in range(U)]
        rows = [sb(f"rows{u}", [P, T, RW]) for u in range(U)]
        onehot = sb("onehot", [P, T * P], bf16)
        hi_b = onehot[:, 0:EPP]
        eae_s = in_node_buf(0, [2, TG * P // 2], G * F_EDGE)
        eae = in_node_buf(TG * P, [2, TG * P // 2], G * F_EDGE)
        dstc = [sb(f"dstc{u}", [P, T + 1]) for u in range(U)]
        hic = [sb(f"hic{u}", [P, T]) for u in range(U)]
        loc = [sb(f"loc{u}", [P, T]) for u in range(U)]
        sign_hi = hi_f[:, 0:T * P // 2].bitcast(bf16).rearrange("p (t m) -> p t m", m=P)
        sign_lo = hi_f[:, T * P // 2:T * (P + NPP) // 2].bitcast(bf16).rearrange("p (t m) -> p t m", m=NPP)
        pen = sb("pen", [P, T])
        etc = sb("etc", [P, T])
        emask = sb("emask", [P, T, N_EDGE_TYPES])
        escore = sb("escore", [P, T])
        pick = h[:].rearrange("p n f -> p (n f)")[:, 0:T * NPP].rearrange("p (t n) -> p t n", n=NPP)
        dscore = sb("dscore", [P, T])
        msg = in_node_buf(2 * TG * P, [T, VW])
        alpha = sb("alpha", [P, T])
        mrun = sb("mrun", [P, T + 1])
        args = sb("args", [P, 2, T])
        wts = sb("wts", [P, 2, T])
        terms = in_node_buf(2 * TG * P + T * VW, [VW, T + 1])
        keep = sb("keep", [P, VW, T + 1])
        sums = sb("sums", [P, VW, T + 1])
        sel_code = sb("sel_code", [P, SEL], mybir.dt.float16)
        sel_node = sb("sel_node", [P, SEL])
        code_sb = [dst_f[:, (NG + u) * (TSM * P // 2):(NG + u + 1) * (TSM * P // 2)].bitcast(mybir.dt.float16)
                   for u in range(U)]
        sel_onehot = dst_f[:, 0:NG * TSM * P // 2].bitcast(bf16).rearrange("p (g e) -> p g e", g=NG)
        sel_mask = sb("sel_mask", [P, TSM, GN])
        sel_prod = h[:].rearrange("p n f -> p (n f)")[:, T * NPP:T * NPP + VW * GN].rearrange("p (f n) -> p f n", n=GN)
        table_group = [table[:, g * GN:(g + 1) * GN, 0:VW].rearrange("p n f -> p f n") for g in range(NG)]
        part_rest = [b[:].rearrange("p a b -> p (a b)")[:, 0:VW * GN].rearrange("p (f n) -> p f n", n=GN)
                     for b in (*rows, *hm)]

        def part_of(k, g):
            return parts[:, k, g, :].rearrange("p (f n) -> p f n", n=GN)

        sel_tmp = [h[:].rearrange("p n f -> p (n f)")[:, k * 2 * SEL:(k + 1) * 2 * SEL] for k in range(3)]

        differ = sb("differ", [P, P], bf16)
        sign_sums = sb("sign_sums", [P, NPP])
        sign_parts = sb("sign_parts", [P, 3, NPP], bf16)
        cnt = sb("cnt", [P, NPP])
        pos = sb("pos", [P, NPP], i32)
        redge_i = sb("redge_i", [P, 4], i32)
        redge = sb("redge", [P, 4])
        rlast_i = sb("rlast_i", [P, P], i32)
        rlast = sb("rlast", [P, P])
        head = sb("head", [P, 8])
        head_idx = sb("head_idx", [P, 2], i32)
        own = sb("own", [P, RW])
        tails = sb("tails", [P, RW])
        contrib = sb("contrib", [P, P])
        mtail = sb("mtail", [P, P])
        wtail = sb("wtail", [P, P])
        wtailT = sb("wtailT", [P, P])
        fix = sb("fix", [P, 4])
        joined = sb("joined", [P, RW])
        scale = sb("scale", [P, 2, NPP])

        falls = sb("falls", [P, 2])
        unsorted = sb("unsorted", [P, 1])
        unsorted_i = sb("unsorted_i", [P, 1], i32)
        before_me = sb("before_me", [P, P])
        tile_rows = sb("tile_rows", [P, RW])
        next_row = sb("next_row", [P, 2])
        mg = sb("mg", [P, 8])
        merge_idx = sb("merge_idx", [P, 2], i32)

        def bank(name, n=1):
            return ctx.enter_context(nc.psum_tensor(name, [P, n, 512], fp32))

        ps_attr = bank("ps_attr", 2)
        ps_msg = bank("ps_msg", 2)
        ps_pick = bank("ps_pick", 2)
        ps_misc = bank("ps_misc", 2)
        ps_sel = ps_misc
        ps_signs = ps_msg[:, 1, 2 * G * VW:2 * G * VW + NPP]
        ps_hmT = [ps_attr, ps_pick]

        weights_in = sem("weights_in")
        zeroed = sem("zeroed")
        diag_in = sem("diag_in")
        x_in = sem("x_in")
        dst_in = sem("dst_in")
        consts = sem("consts")
        dve_step = sem("dve_step")
        signs_ready = sem("signs_ready")
        signs_mm = sem("signs_mm")
        signs_summed = sem("signs_summed")
        places_ready = sem("places_ready")
        sign_parts_ready = sem("sign_parts_ready")
        differ_mm = sem("differ_mm")
        node_w_mm = sem("node_w_mm")
        node_w_sb = sem("node_w_sb")
        node_b7_ready = sem("node_b7_ready")
        maskT_sb = sem("maskT_sb")
        head_counted = sem("head_counted")
        var_ready = sem("var_ready")
        dev_ready = sem("dev_ready")
        zeros_ready = sem("zeros_ready")
        hm_ready = sem("hm_ready")
        hmT_mm = sem("hmT_mm")
        hmT_sb = sem("hmT_sb")
        tab_mm = sem("tab_mm")
        tab_sb = sem("tab_sb")
        table_out = sem("table_out")
        dst_used = sem("dst_used")
        hi_ready = sem("hi_ready")
        hi_out = sem("hi_out")
        s_parts = sem("s_parts")
        sel_in = sem("sel_in")
        codes_ready = sem("codes_ready")
        codes_out = sem("codes_out")
        code_in = [sem(f"code_in{u}") for u in range(U)]
        sel_first_ready = sem("sel_first_ready")
        sel_onehot_ready = sem("sel_onehot_ready")
        part_copied = sem("part_copied")
        rest_ready = sem("rest_ready")
        parts_ready = sem("parts_ready")
        sel_mm = sem("sel_mm")
        sel_read = sem("sel_read")
        gather_turns = sem("gather_turns")
        meta_in = [sem(f"meta_in{u}") for u in range(U)]
        attr_in = [sem(f"attr_in{u}") for u in range(U)]
        hib_in = [sem(f"hib_in{u}") for u in range(U)]
        gathered = [sem(f"gathered{u}") for u in range(U)]
        stored = [sem(f"stored{u}") for u in range(U)]
        attr_mm = sem("attr_mm")
        eae_scaled = sem("eae_scaled")
        eae_ready = sem("eae_ready")
        msg_mm = sem("msg_mm")
        msg_added = sem("msg_added")
        onehot_ready = sem("onehot_ready")
        pick_mm = sem("pick_mm")
        picked = sem("picked")
        args_ready = sem("args_ready")
        exp_done = sem("exp_done")
        keep_ready = sem("keep_ready")
        sums_ready = sem("sums_ready")
        rows_sums = sem("rows_sums")
        head_idx_ready = sem("head_idx_ready")
        own_in = sem("own_in")
        tails_in = sem("tails_in")
        mtail_mm = sem("mtail_mm")
        targs_ready = sem("targs_ready")
        texp_done = sem("texp_done")
        wtailT_mm = sem("wtailT_mm")
        wtailT_sb = sem("wtailT_sb")
        tsum_mm = sem("tsum_mm")
        joined_ready = sem("joined_ready")
        falls_ready = sem("falls_ready")
        falls_mm = sem("falls_mm")
        unsorted_ready = sem("unsorted_ready")
        pos_ready = sem("pos_ready")
        join_step = sem("join_step")
        merge_step = sem("merge_step")
        last_step = sem("last_step")
        node_rows_ready = sem("node_rows_ready")
        node_rows_out = sem("node_rows_out")
        sp_turns = sem("sp_turns")
        tile_in = sem("tile_in")
        merge_keys = sem("merge_keys")
        merge_keys_mm = sem("merge_keys_mm")
        merge_idx_ready = sem("merge_idx_ready")
        node_in = sem("node_in")
        merge_args = sem("merge_args")
        merge_exp = sem("merge_exp")
        merge_wT_mm = sem("merge_wT_mm")
        merge_wT_sb = sem("merge_wT_sb")
        merge_sum_mm = sem("merge_sum_mm")
        merge_row_ready = sem("merge_row_ready")
        merge_out = sem("merge_out")
        joined_out = sem("joined_out")
        last_in = [sem(f"last_in{k}") for k in range(2)]
        out_ready = sem("out_ready")
        out_done = sem("out_done")

        def count(n):
            return n + 1

        def selected(i, u):
            return i * TS_ITER + TS_BEFORE[u]

        def start_at_one(eng, *sems):
            for s in sems:
                eng.sem_inc(s, 1)

        def is_unsorted(eng):
            eng.wait_ge(unsorted_ready, 1)
            return eng.value_load(unsorted_i[0:1, 0:1], min_val=0, max_val=1)

        block = ctx.enter_context(nc.Block())

        @block.sync
        def _(sp):
            def load_hib(c, u):
                sp.dma_start(hib_sb[u][:], dst_hi_dram[ds(c, 1), :].rearrange("a e -> (a e)")
                             .partition_broadcast(P)).then_inc(hib_in[u], 16)

            def load_code(c, u):
                sp.dma_start(code_sb[u], sel_code_dram[ds(c, 1), :].rearrange("a e -> (a e)")
                             .partition_broadcast(P)).then_inc(code_in[u], 16)

            def load_attr(c, u):
                sp.dma_start(attr_sb[u][:], edge_attr_t[:, ds(c, 1), :].rearrange("k a m -> k (a m)")).then_inc(
                    attr_in[u], 16)

            sp.dma_start(x_sb, x).then_inc(x_in, 16)
            sp.dma_start(ntype[:], node_type).then_inc(x_in, 16)
            for dst, src in ((scores_w[:, 0:F_IN], lin_w[0:F_IN, :]),
                             (scores_w[:, F_IN:F_IN + 1], att_w[F_IN:2 * F_IN, :]),
                             (scores_w[:, F_IN + 1:F_IN + 2], att_w[0:F_IN, :]),
                             (het_wT[:], hetero_wT), (het_bT[:], hetero_bT),
                             (emb[:], edge_type_emb.partition_broadcast(P)),
                             (att_type[:], att_w[2 * F_IN:2 * F_IN + F_EDGE, 0].partition_broadcast(P)),
                             (redge_i[:], row_edges), (rlast_i[:], row_last.partition_broadcast(P))):
                sp.dma_start(dst, src).then_inc(weights_in, 16)
            sp.dma_start(dst_i, dst_tmajor).then_inc(dst_in, 16)
            for u in range(U):
                sp.dma_start(meta_sb[u][:], meta[:, u, :]).then_inc(meta_in[u], 16)
            sp.wait_ge(zeroed, 2)
            for g in range(G):
                k = slice(g * F_EDGE, (g + 1) * F_EDGE)
                sp.dma_start(attr_w[k, k], edge_attr_w).then_inc(diag_in, 16)
                sp.dma_start(msg_w[k, g * VW:g * VW + F_IN], lin_w[F_IN:F_IN + F_EDGE, :]).then_inc(diag_in, 16)
                sp.dma_start(msg_w[k, g * VW + F_IN:(g + 1) * VW],
                             att_w[2 * F_IN + F_EDGE:2 * F_IN + 2 * F_EDGE, :]).then_inc(diag_in, 16)
            for u in range(U):
                load_attr(u, u)
            sp.wait_ge(tab_sb, NODE_ITERS + 2)
            sp.dma_start(table_dram.rearrange("(p n) f -> p n f", p=P), table).then_inc(table_out, 16)
            sp.wait_ge(dst_used, 1)
            sp.dma_start(dst_f[:].bitcast(i32), dst_rows).then_inc(dst_in, 16)
            sp.wait_ge(hi_ready, 1)
            sp.dma_start(dst_hi_dram.rearrange("c (a b) -> (c a b)", a=1).rearrange("(p e) -> p e", p=P),
                         hi_b).then_inc(hi_out, 16)
            sp.dma_start(sel_tmp[0].bitcast(i32), sel_src).then_inc(sel_in, 16)
            sp.wait_ge(hi_out, 16)
            for u in range(U):
                load_hib(u, u)
            sp.wait_ge(codes_ready, 1)
            sp.dma_start(sel_code_dram.rearrange("c (a b) -> (c a b)", a=1).rearrange("(p e) -> p e", p=P),
                         sel_code[:]).then_inc(codes_out, 16)
            sp.wait_ge(codes_out, 16)
            sp.wait_ge(head_counted, 1)
            for u in range(U):
                load_code(u, u)
            sp.wait_ge(node_rows_ready, 1)
            sp.dma_start(node_rows, tile_rows[:].unsqueeze(1).broadcast_to([P, NPP, RW])).then_inc(node_rows_out, 16)
            with sp.Fori(1, ITERS) as i:
                for u in range(U):
                    sp.wait_ge(sums_ready, count(i * U + u + 1 - U))
                    sp.dma_start(meta_sb[u][:], meta[:, ds(i * U + u, 1), :].rearrange("p a m -> p (a m)")).then_inc(
                        meta_in[u], 16)
                    load_hib(i * U + u, u)
                    load_code(i * U + u, u)
                    load_attr(i * U + u, u)
            for u in range(U):
                sp.wait_ge(stored[u], 16 * ITERS + 1)
            flag = is_unsorted(sp)
            sp.wait_ge(sel_mm, count(ITERS * TS_ITER))
            sp.dma_start(x_sb, x).then_inc(x_in, 16)
            with sp.If(flag < 1):
                sp.dma_start(tails[:], rows_pm[:, EPP - 1, :]).then_inc(tails_in, 16)
                sp.wait_ge(tails_in, 16)
            with sp.If(flag >= 1):
                sp.wait_ge(node_rows_out, 16)
                with sp.Fori(0, EPP) as t:
                    sp.dma_start(tile_rows[:], rows_pm[:, ds(t, 1), :].rearrange("p a f -> p (a f)")).then_inc(
                        tile_in, 16)
                    sp.dma_start(next_row[:], rows_after[:, ds(t, 1), VW:RW].rearrange("p a f -> p (a f)")).then_inc(
                        tile_in, 16)
                    sp.wait_ge(merge_row_ready, t + 1)
                    sp.sem_inc(sp_turns, 1)
            for k, n in enumerate((slice(0, PIECE), slice(PIECE, NPP))):
                sp.wait_ge(out_ready, k + 1)
                sp.dma_start(out[:, n, :], h[:, n, :]).then_inc(out_done, 16)
            sp.wait_ge(out_done, 32)
            sp.wait_ge(table_out, 16)

        @block.gpsimd
        def _(pool):
            nc.gpsimd.memset(attr_w[:], 0.0).then_inc(zeroed, 1)
            nc.gpsimd.memset(msg_w[:], 0.0).then_inc(zeroed, 1)
            nc.gpsimd.memset(ident[:], 0.0).then_inc(consts, 1)
            pool.wait_ge(consts, 1)
            nc.gpsimd.affine_select(out=ident[:], in_=ident[:], compare_op=ALU.not_equal, fill=1.0, base=0,
                                    pattern=[[-1, P]], channel_multiplier=1).then_inc(consts, 1)
            for tile, base, step, mult in ((part, 0, 0, 1), (free98, 0, 1, 0), (free128, 0, 1, 0),
                                           (node_id, 0, 1, NPP), (types8, 0, 1, 0),
                                           (group_row, 0, -N_NODE_TYPES, 1),
                                           (part_group, 0, P, 1)):
                nc.gpsimd.iota(tile[:], [[step, tile.shape[1]]], base=base, channel_multiplier=mult,
                               allow_small_or_imprecise_dtypes=True).then_inc(consts, 1)
            pool.wait_ge(table_out, 16)
            with pool.Fori(0, ITERS) as i:
                for u in range(U):
                    pool.wait_ge(meta_in[u], (i + 1) * 16)
                    pool.sem_inc(gather_turns, 1)
                    for t in range(T - TS[u]):
                        nc.gpsimd.indirect_dma_start(
                            gath[u][:, t, :], None, table_dram,
                            bass.IndirectOffsetOnAxis(ap=meta_sb[u][:, t:t + 1], axis=0)).then_inc(gathered[u], 16)
            for u in range(U):
                pool.wait_ge(stored[u], 16 * ITERS + 1)
            flag = is_unsorted(pool)
            with pool.If(flag < 1):
                pool.wait_ge(head_idx_ready, 1)
                nc.gpsimd.indirect_dma_start(own[:], None, rows_dram,
                                             bass.IndirectOffsetOnAxis(ap=head_idx[:, 0:1], axis=0)).then_inc(own_in, 16)
                pool.wait_ge(joined_ready, 1)
                nc.gpsimd.indirect_dma_start(rows_dram, bass.IndirectOffsetOnAxis(ap=head_idx[:, 1:2], axis=0),
                                             joined[:], None, bounds_check=N_EDGES - 1, oob_is_err=False).then_inc(
                    joined_out, 16)
                pool.wait_ge(joined_out, 16)
            with pool.If(flag >= 1):
                pool.wait_ge(node_rows_out, 16)
                with pool.Fori(0, EPP) as t:
                    pool.wait_ge(merge_idx_ready, t + 1)
                    pool.sem_inc(gather_turns, 1)
                    nc.gpsimd.indirect_dma_start(
                        own[:], None, rows_dram,
                        bass.IndirectOffsetOnAxis(ap=merge_idx[:, 0:1], axis=0)).then_inc(node_in, 16)
                    pool.wait_ge(merge_row_ready, t + 1)
                    pool.sem_inc(gather_turns, 1)
                    nc.gpsimd.indirect_dma_start(
                        rows_dram, bass.IndirectOffsetOnAxis(ap=merge_idx[:, 1:2], axis=0), joined[:], None,
                        bounds_check=N_EDGES + N_PAD - 1, oob_is_err=False).then_inc(merge_out, 16)
                    pool.wait_ge(merge_out, t * 16 + 16)
                    pool.sem_inc(gather_turns, 1)
            pool.wait_ge(pos_ready, 1)
            pool.wait_ge(node_rows_out, 16)
            for n in range(NPP):
                nc.gpsimd.indirect_dma_start(
                    last_rows[:, n, :], None, rows_dram,
                    bass.IndirectOffsetOnAxis(ap=pos[:, n:n + 1], axis=0)).then_inc(last_in[n >= PIECE], 16)

        @block.scalar
        def _(act):
            start_at_one(act, hmT_sb, rows_sums, *stored)
            act.wait_ge(node_w_mm, 1)
            nc.scalar.copy(node_w[:], ps_misc[:, 0, 0:YW])
            nc.scalar.copy(node_b[:], ps_misc[0:MB, 0, YW:2 * YW]).then_inc(node_w_sb, 1)
            act.wait_ge(var_ready, 1)
            nc.scalar.sqrt(stat[:, 3, :], stat[:, 2, :]).then_inc(dev_ready, 1)
            with act.Fori(0, NODE_ITERS // 2) as i:
                for k in range(2):
                    n = i * 2 + k
                    act.wait_ge(hmT_mm, n + 1)
                    act.wait_ge(tab_mm, n + 1)
                    for b, w in enumerate((4 * P, 3 * P)):
                        last = nc.scalar.copy(hmT[k][:, b * 4 * P:b * 4 * P + w], ps_hmT[k][:, b, 0:w])
                    last.then_inc(hmT_sb, 1)
            act.wait_ge(tab_sb, NODE_ITERS + 2)
            for g in range(NG):
                nc.scalar.copy(part_of(0, g), table_group[g]).then_inc(part_copied, 1)
            for g in range(NG):
                act.wait_ge(rest_ready, g + 1)
                nc.scalar.copy(part_of(1, g), part_rest[g]).then_inc(part_copied, 1)
            for g in range(NG):
                act.wait_ge(rest_ready, NG + g + 1)
                last = nc.scalar.copy(part_of(2, g), part_rest[g])
            last.then_inc(parts_ready, 1)
            act.wait_ge(parts_ready, 1)
            act.wait_ge(head_counted, 1)
            act.wait_ge(table_out, 16)

            def scale_attr(c):
                act.wait_ge(attr_mm, c + 1)
                act.wait_ge(eae_ready, count(c))
                nc.scalar.mul(eae_s, ps_attr[0:G * F_EDGE, :, 0:TG * P // 2], SLOPE).then_inc(eae_scaled, 1)

            def chunk(i, u, final):
                c = i * U + u
                act.wait_ge(places_ready, c + 1)
                act.wait_ge(signs_mm, count(c))
                for t in range(T):
                    nc.scalar.activation(sign_hi[:, t, :], half128[:], ACT.Sign, bias=hic[u][:, t:t + 1],
                                         scale=-1.0)
                    last = nc.scalar.activation(sign_lo[:, t, :], half128[:, 0:NPP], ACT.Sign,
                                                bias=loc[u][:, t:t + 1], scale=-1.0)
                last.then_inc(signs_ready, 1)
                act.wait_ge(args_ready, c + 1)
                nc.scalar.activation(wts[:], args[:], ACT.Exp).then_inc(exp_done, 1)
                act.wait_ge(stored[u], i * 16 + 1)
                nc.scalar.copy(rows[u][:, :, VW], mrun[:, 1:T + 1])
                nc.scalar.copy(rows[u][:, :, VW + 1], dstc[u][:, 1:T + 1])
                act.wait_ge(exp_done, c + 1)
                act.wait_ge(sums_ready, count(c))
                nc.scalar.copy(keep[:, :, 1:T + 1], wts[:, 1:2, :].broadcast_to([P, VW, T])).then_inc(
                    keep_ready, 1)
                if not final:
                    scale_attr(c + 1)
                act.wait_ge(sums_ready, count(c + 1))
                nc.scalar.copy(rows[u][:, :, 0:VW], sums[:, :, 1:T + 1].rearrange("p f t -> p t f")).then_inc(
                    rows_sums, 1)
                act.wait_ge(rows_sums, count(c + 1))
                act.dma_start(rows_pm[:, ds(c * T, T), :], rows[u][:]).then_inc(stored[u], 16)

            scale_attr(0)
            with act.Fori(0, ITERS - 1) as i:
                for u in range(U):
                    chunk(i, u, False)
            for u in range(U):
                chunk(ITERS - 1, u, u == U - 1)
            flag = is_unsorted(act)
            with act.If(flag < 1):
                act.wait_ge(targs_ready, 1)
                nc.scalar.activation(wtail[:], mtail[:], ACT.Exp)
                nc.scalar.activation(fix[:, 2:3], fix[:, 1:2], ACT.Exp).then_inc(texp_done, 1)
            with act.If(flag >= 1):
                with act.Fori(0, EPP) as t:
                    act.wait_ge(merge_args, t + 1)
                    nc.scalar.activation(wtail[:], mtail[:], ACT.Exp)
                    nc.scalar.activation(fix[:, 2:3], fix[:, 1:2], ACT.Exp).then_inc(merge_exp, 1)

        @block.tensor
        def _(pe):
            pe.sem_inc(tab_mm, 2)
            start_at_one(pe, pick_mm, msg_mm, sel_mm, signs_mm)
            pe.wait_ge(weights_in, 9 * 16)
            nc.tensor.matmul(ps_misc[:, 0, 0:YW], het_wT[:], scores_w[:], start=True, stop=True)
            pe.wait_ge(node_b7_ready, 1)
            nc.tensor.matmul(ps_misc[0:MB, 0, YW:2 * YW], het_bT7[:].rearrange("f a b -> f (a b)"), scores_w[:],
                             start=True, stop=True).then_inc(node_w_mm, 1)
            pe.wait_ge(consts, 2)
            pe.wait_ge(node_w_sb, 1)
            pe.wait_ge(node_b7_ready, 2)

            def transposes(n, k):
                pe.wait_ge(hm_ready, n + 1)
                if not isinstance(n, int) or n:
                    pe.wait_ge(hmT_sb, n)
                    pe.wait_ge(maskT_sb, n)
                nc.tensor.transpose(ps_msg[0:MB, k, 0:P], hmask[k][:], ident[:])
                for j in range(N7):
                    last = nc.tensor.transpose(ps_hmT[k][:, j // 4, j % 4 * P:(j % 4 + 1) * P], hm[k][:, j, :],
                                               ident[:])
                last.then_inc(hmT_mm, 1)

            def products(n, k):
                pe.wait_ge(hmT_sb, count(n + 1))
                pe.wait_ge(maskT_sb, count(n + 1))
                pe.wait_ge(tab_sb, n + 1)
                nc.tensor.matmul(ps_misc[:, k, 0:N7 * YW], maskT[k][:], node_b7[:].rearrange("p a b -> p (a b)"),
                                 start=True, stop=False)
                for j in range(N7):
                    last = nc.tensor.matmul(ps_misc[:, k, j * YW:(j + 1) * YW], hmT[k][:, j * P:(j + 1) * P],
                                            node_w[:], start=False, stop=(j == N7 - 1))
                last.then_inc(tab_mm, 1)

            pe.wait_ge(zeros_ready, 1)
            pe.wait_ge(dev_ready, 1)
            zeros = sums[:].rearrange("p f t -> p (f t)").bitcast(bf16)
            for _ in range(WARM_UP):
                nc.tensor.matmul(ps_pick[:, 0, 0:512], zeros[:, 0:P], zeros[:, 0:512], start=True, stop=True)

            transposes(0, 0)
            with pe.Fori(0, NODE_ITERS // 2 - 1) as i:
                transposes(i * 2 + 1, 1)
                products(i * 2, 0)
                transposes(i * 2 + 2, 0)
                products(i * 2 + 1, 1)
            transposes(NODE_ITERS - 1, 1)
            products(NODE_ITERS - 2, 0)
            products(NODE_ITERS - 1, 1)
            pe.wait_ge(falls_ready, 1)
            nc.tensor.matmul(ps_misc[:, 0, 0:1], before_me[:], falls[:, 0:1], start=True, stop=True).then_inc(
                falls_mm, 1)
            pe.wait_ge(s_parts, 1)
            pe.wait_ge(diag_in, 3 * G * 16)

            def select(i, u, j):
                pe.wait_ge(sel_onehot_ready if j else sel_first_ready, i * U + u + 1)
                pe.wait_ge(sel_read, count(selected(i, u) + (j - 1 if j > 1 else 0)))
                for g in range(NG):
                    for k in range(3):
                        last = nc.tensor.matmul(ps_sel[:, j % 2, 0:VW * GN], sel_onehot[:, g, j * P:(j + 1) * P],
                                                parts[:, k, g, :], start=(g == 0 and k == 0),
                                                stop=(g == NG - 1 and k == 2))
                last.then_inc(sel_mm, 1)

            def dst_scores(c, g):
                pe.wait_ge(onehot_ready, c + 1)
                pe.wait_ge(picked, count((c * TG + (g - 1 if g else 0)) * G))
                for j in range(G):
                    t = g * G + j
                    for k in range(3):
                        last = nc.tensor.matmul(ps_pick[:, g % 2, j * NPP:(j + 1) * NPP],
                                                onehot[:, t * P:(t + 1) * P], s_dst[:, k, :],
                                                start=(k == 0), stop=(k == 2))
                last.then_inc(pick_mm, 1)

            def attr_product(i, u):
                pe.wait_ge(attr_in[u], (i + 1) * 16)
                for b in range(2):
                    last = nc.tensor.matmul(ps_attr[0:G * F_EDGE, b, 0:TG * P // 2], attr_w[:],
                                            attr_sb[u][:, b * (TG * P // 2):(b + 1) * (TG * P // 2)],
                                            start=True, stop=True)
                last.then_inc(attr_mm, 1)

            def chunk(i, u, final):
                c = i * U + u
                after = (i if u < U - 1 else i + 1, (u + 1) % U)
                dst_scores(c, 0)
                dst_scores(c, 1)
                if not final:
                    select(*after, 0)
                dst_scores(c, 2)
                dst_scores(c, 3)
                pe.wait_ge(eae_ready, count(c + 1))
                if not final:
                    attr_product(*after)
                pe.wait_ge(msg_added, count(c))
                pe.wait_ge(signs_summed, count(c + 1))
                eae_flat = eae.rearrange("k a b -> k (a b)")
                for g in range(TG):
                    last = nc.tensor.matmul(ps_msg[:, g // 3, g % 3 * G * VW:(g % 3 + 1) * G * VW],
                                            eae_flat[:, g * P:(g + 1) * P], msg_w[:], start=True, stop=True)
                last.then_inc(msg_mm, 1)
                dst_scores(c, 4)
                if not final:
                    select(*after, 1)
                    select(*after, 2)
                pe.wait_ge(signs_ready, c + 1)
                pe.wait_ge(msg_added, count(c + 1))
                for t in range(T):
                    last = nc.tensor.matmul(ps_signs, sign_hi[:, t, :], sign_lo[:, t, :], start=(t == 0),
                                            stop=(t == T - 1))
                last.then_inc(signs_mm, 1)
                if not final:
                    for j in range(3, TS[after[1]]):
                        select(*after, j)

            attr_product(0, 0)
            pe.wait_ge(parts_ready, 1)
            for j in range(TS[0]):
                select(0, 0, j)
            with pe.Fori(0, ITERS - 1) as i:
                for u in range(U):
                    chunk(i, u, False)
            for u in range(U):
                chunk(ITERS - 1, u, u == U - 1)
            pe.wait_ge(sign_parts_ready, 1)
            for k in range(3):
                last = nc.tensor.matmul(ps_misc[:, 1, 0:NPP], differ[:], sign_parts[:, k, :], start=(k == 0),
                                        stop=(k == 2))
            last.then_inc(differ_mm, 1)
            flag = is_unsorted(pe)
            with pe.If(flag < 1):
                pe.wait_ge(tails_in, 16)
                pe.wait_ge(head_idx_ready, 1)
                nc.tensor.transpose(ps_misc[:, 0, 0:P], mtail[:], ident[:]).then_inc(mtail_mm, 1)
                pe.wait_ge(texp_done, 1)
                nc.tensor.transpose(ps_misc[:, 0, P:2 * P], wtail[:], ident[:]).then_inc(wtailT_mm, 1)
                pe.wait_ge(wtailT_sb, 1)
                nc.tensor.matmul(ps_misc[:, 0, 2 * P:2 * P + VW], wtailT[:], tails[:, 0:VW], start=True,
                                 stop=True).then_inc(tsum_mm, 1)
            with pe.If(flag >= 1):
                with pe.Fori(0, EPP) as t:
                    pe.wait_ge(merge_keys, t + 1)
                    nc.tensor.transpose(ps_misc[:, 0, 0:P], mtail[:], ident[:])
                    nc.tensor.transpose(ps_misc[:, 0, P:2 * P], contrib[:], ident[:]).then_inc(merge_keys_mm, 1)
                    pe.wait_ge(merge_exp, t + 1)
                    nc.tensor.transpose(ps_misc[:, 1, 0:P], wtail[:], ident[:]).then_inc(merge_wT_mm, 1)
                    pe.wait_ge(merge_wT_sb, t + 1)
                    nc.tensor.matmul(ps_misc[:, 1, 2 * P:2 * P + VW], wtailT[:], tile_rows[:, 0:VW], start=True,
                                     stop=True).then_inc(merge_sum_mm, 1)

        @block.vector
        def _(dve):
            v = nc.vector
            dve.sem_inc(tab_sb, 2)
            start_at_one(dve, maskT_sb, eae_ready, signs_summed, picked, msg_added, sums_ready, sel_read)
            steps = [0]

            def done(ins, at=0):
                steps[0] += 1
                ins.then_inc(dve_step, 1)
                dve.wait_ge(dve_step, at + steps[0])

            def step(ins):
                steps[0] += 1
                ins.then_inc(dve_step, 1)
                return steps[0]

            def need(k, at):
                dve.wait_ge(dve_step, at + k)

            def stage(own_steps):
                taken = [0]

                def stage_done(ins, at=0):
                    taken[0] += 1
                    ins.then_inc(own_steps, 1)
                    dve.wait_ge(own_steps, at + taken[0])
                return stage_done

            placed = [0]

            def place(n, i, u, at=0):
                if n == 0:
                    dve.wait_ge(meta_in[u], (i + 1) * 16)
                    placed[0] = step(v.tensor_copy(dstc[u][:], meta_sb[u][:, T:2 * T + 1]))
                    return
                need(placed[0], at)
                if n == 1:
                    placed[0] = step(v.tensor_scalar(hic[u][:], dstc[u][:, 1:T + 1], 1.0 / NPP, 0.5 / NPP - 0.5,
                                                     ALU.mult, ALU.add))
                elif n == 2:
                    placed[0] = step(v.tensor_scalar(hic[u][:], hic[u][:], ROUND, ROUND, ALU.add, ALU.subtract))
                else:
                    v.scalar_tensor_tensor(loc[u][:], hic[u][:], -float(NPP), dstc[u][:, 1:T + 1], ALU.mult,
                                           ALU.add).then_inc(places_ready, 1)

            v.memset(keep[:, :, 0:1], 0.0)
            v.memset(sums[:], 0.0).then_inc(zeros_ready, 1)
            v.memset(sign_sums[:], 0.0)
            v.memset(tile_rows[:, 0:VW], 0.0)
            v.memset(tile_rows[:, VW:VW + 1], -BIG)
            v.memset(tile_rows[:, VW + 1:RW], -1.0).then_inc(node_rows_ready, 1)
            v.memset(ps_signs, 0.0)
            done(v.memset(mrun[:], 0.0))
            dve.wait_ge(weights_in, 9 * 16)
            v.tensor_copy(het_bT7[:], het_bT[:].unsqueeze(1).broadcast_to([F_IN, N7, N_NODE_TYPES])).then_inc(
                node_b7_ready, 1)
            dve.wait_ge(x_in, 32)
            sq = table[:, :, 0:F_IN]
            done(v.tensor_reduce(stat[:, 0, :], x_sb, AX.X, ALU.add))
            done(v.tensor_scalar(stat[:, 1, :], stat[:, 0, :], 1.0 / F_IN, None, ALU.mult))
            done(v.tensor_tensor(h[:], x_sb, stat[:, 1, :].unsqueeze(2).broadcast_to([P, NPP, F_IN]), ALU.subtract))
            done(v.tensor_tensor(sq, h[:], h[:], ALU.mult))
            done(v.tensor_reduce(stat[:, 0, :], sq, AX.X, ALU.add))
            v.tensor_scalar(stat[:, 2, :], stat[:, 0, :], 1.0 / F_IN, 1e-5, ALU.mult, ALU.add).then_inc(var_ready, 1)
            done(v.tensor_copy(ntype_f[:], ntype[:]))
            dve.wait_ge(consts, 9)
            done(v.tensor_tensor(tmask[:], ntype_f[:].unsqueeze(2).broadcast_to([P, NPP, N_NODE_TYPES]),
                                 types8[:, 0:N_NODE_TYPES].unsqueeze(1).broadcast_to([P, NPP, N_NODE_TYPES]),
                                 ALU.is_equal))
            dve.wait_ge(dev_ready, 1)
            done(v.reciprocal(stat[:, 0, :], stat[:, 3, :]))
            done(v.scalar_tensor_tensor(h[:], h[:], 0.0, stat[:, 0, :].unsqueeze(2).broadcast_to([P, NPP, F_IN]),
                                        ALU.max, ALU.mult))
            done(v.tensor_scalar(group_sel[:], group_row[:], 0.0, None, ALU.is_ge))
            done(v.scalar_tensor_tensor(group_sel[:], group_row[:], float(N_NODE_TYPES - 1), group_sel[:], ALU.is_le,
                                        ALU.mult))
            dve.wait_ge(node_w_sb, 1)
            v.tensor_tensor(node_b7[:], node_b[:].unsqueeze(1).broadcast_to([MB, N7, YW]),
                            group_sel[:].unsqueeze(2).broadcast_to([MB, N7, YW]), ALU.mult).then_inc(node_b7_ready, 1)

            def by_type(n, k):
                v.tensor_tensor(hm[k][:].rearrange("p n (k f) -> p n k f", f=F_IN),
                                h[:, ds(n * N7, N7), :].unsqueeze(2).broadcast_to([P, N7, N_NODE_TYPES, F_IN]),
                                tmask[:, ds(n * N7, N7), :].unsqueeze(3).broadcast_to([P, N7, N_NODE_TYPES, F_IN]),
                                ALU.mult)
                v.tensor_copy(hmask[k][:].rearrange("p (n k) -> p n k", k=N_NODE_TYPES),
                              tmask[:, ds(n * N7, N7), :]).then_inc(hm_ready, 1)

            def from_psum(n, k):
                dve.wait_ge(hmT_mm, n + 1)
                dve.wait_ge(tab_mm, n + 1)
                v.tensor_copy(maskT[k][:], ps_msg[0:MB, k, 0:P]).then_inc(maskT_sb, 1)

            def table_rows(n, k):
                dve.wait_ge(tab_mm, n + 3)
                v.tensor_scalar(table[:, ds(n * N7, N7), :],
                                ps_misc[:, k, 0:N7 * YW].rearrange("p (n f) -> p n f", f=YW), 1.0, None,
                                ALU.mult).then_inc(tab_sb, 1)

            by_type(0, 0)
            by_type(1, 1)
            with dve.Fori(0, NODE_ITERS // 2 - 1) as i:
                from_psum(i * 2, 0)
                from_psum(i * 2 + 1, 1)
                by_type(i * 2 + 2, 0)
                table_rows(i * 2, 0)
                by_type(i * 2 + 3, 1)
                table_rows(i * 2 + 1, 1)
            from_psum(NODE_ITERS - 2, 0)
            from_psum(NODE_ITERS - 1, 1)
            def div98(to, src):
                done(v.tensor_scalar(to, src, 1.0 / NPP, 0.5 / NPP - 0.5, ALU.mult, ALU.add))
                done(v.tensor_scalar(to, to, ROUND, ROUND, ALU.add, ALU.subtract))

            dve.wait_ge(dst_in, 16)
            done(v.tensor_copy(dst_f[:], dst_i))
            table_rows(NODE_ITERS - 2, 0)
            table_rows(NODE_ITERS - 1, 1)
            dve.wait_ge(tab_sb, NODE_ITERS + 2)
            score = table[:, :, F_IN + 1]
            done(v.tensor_copy(s_dst[:, 0, :], score))
            done(v.tensor_tensor(s_rest[:], score, s_dst[:, 0, :], ALU.subtract))
            done(v.tensor_copy(s_dst[:, 1, :], s_rest[:]))
            done(v.tensor_tensor(s_rest[:], s_rest[:], s_dst[:, 1, :], ALU.subtract))
            v.tensor_copy(s_dst[:, 2, :], s_rest[:]).then_inc(s_parts, 1)
            v.tensor_scalar(hi_f[:], dst_f[:], 1.0 / NPP, 0.5 / NPP - 0.5, ALU.mult, ALU.add).then_inc(dst_used, 1)
            dve.wait_ge(dst_used, 1)
            done(v.tensor_scalar(hi_f[:], hi_f[:], ROUND, ROUND, ALU.add, ALU.subtract))
            v.tensor_copy(hi_b, hi_f[:]).then_inc(hi_ready, 1)
            for g in range(NG):
                dve.wait_ge(part_copied, g + 1)
                v.tensor_tensor(part_rest[g], table_group[g], part_of(0, g), ALU.subtract).then_inc(rest_ready, 1)
            for g in range(NG):
                dve.wait_ge(part_copied, NG + g + 1)
                v.tensor_tensor(part_rest[g], part_rest[g], part_of(1, g), ALU.subtract).then_inc(rest_ready, 1)
            dve.wait_ge(sel_in, 16)
            group, node, row = sel_tmp
            done(v.tensor_copy(node, group.bitcast(i32)))
            div98(row, node)
            done(v.scalar_tensor_tensor(node, row, -float(NPP), node, ALU.mult, ALU.add))
            done(v.tensor_scalar(group, node, 1.0 / GN, 0.5 / GN - 0.5, ALU.mult, ALU.add))
            done(v.tensor_scalar(group, group, ROUND, ROUND, ALU.add, ALU.subtract))
            v.scalar_tensor_tensor(sel_code[:], group[:, 0:SEL], float(P), row[:, 0:SEL], ALU.mult,
                                   ALU.add).then_inc(codes_ready, 1)
            done(v.scalar_tensor_tensor(sel_node[:], group[:, SEL:2 * SEL], -float(GN), node[:, SEL:2 * SEL], ALU.mult,
                                        ALU.add))
            done(v.scalar_tensor_tensor(emb_act[:], emb[:], SLOPE, emb[:], ALU.mult, ALU.max))
            done(v.tensor_tensor(emb_act[:], emb_act[:], att_type[:].unsqueeze(1).broadcast_to(
                [P, N_EDGE_TYPES, F_EDGE]), ALU.mult))
            done(v.tensor_reduce(type_score[:], emb_act[:], AX.X, ALU.add))

            for n in range(4):
                place(n, 0, 0)
            v.tensor_scalar(half128[:], free128[:], 0.5, None, ALU.add)
            done(v.tensor_scalar(wtail[:], free128[:], part[:, 0:1], None, ALU.subtract))
            v.tensor_scalar(mtail[:], wtail[:], 1.0, None, ALU.is_equal)
            done(v.tensor_scalar(wtailT[:], wtail[:], -(P - 1.0), None, ALU.is_equal))
            done(v.tensor_tensor(mtail[:], wtailT[:], mtail[:], ALU.subtract))
            v.tensor_tensor(differ[:], ident[:], mtail[:], ALU.add)
            done(v.tensor_copy(redge[:], redge_i[:]))
            done(v.tensor_copy(rlast[:], rlast_i[:]))
            dve.wait_ge(dst_in, 32)
            dve.wait_ge(hi_ready, 1)
            done(v.tensor_copy(hi_f[:], dst_f[:].bitcast(i32)))
            v.memset(before_me[:], 1.0)
            done(v.scalar_tensor_tensor(dst_f[:, 0:EPP - 1], hi_f[:, 0:EPP - 1], 1.0, hi_f[:, 1:EPP], ALU.mult,
                                        ALU.is_gt, accum_out=falls[:, 0:1]))
            done(v.tensor_tensor(falls[:, 1:2], redge[:, 2:3], redge[:, 0:1], ALU.is_gt))
            v.tensor_tensor(falls[:, 0:1], falls[:, 0:1], falls[:, 1:2], ALU.add).then_inc(falls_ready, 1)
            dve.wait_ge(falls_mm, 1)
            done(v.tensor_scalar(unsorted[:], ps_misc[:, 0, 0:1], 1.0, None, ALU.min))
            v.tensor_copy(unsorted_i[:], unsorted[:]).then_inc(unsorted_ready, 1)
            v.tensor_scalar(dst_f[:], hi_f[:], redge[:, 0:1], 0.0, ALU.is_equal, ALU.add,
                            accum_out=head[:, 0:1]).then_inc(head_counted, 1)
            dve.wait_ge(head_counted, 1)
            done(v.scalar_tensor_tensor(head[:, 1:2], part[:], float(EPP), head[:, 0:1], ALU.mult, ALU.add))
            done(v.tensor_scalar(head[:, 1:2], head[:, 1:2], -1.0, None, ALU.add))
            done(v.tensor_tensor(head[:, 2:3], redge[:, 0:1], redge[:, 2:3], ALU.is_equal))
            done(v.tensor_tensor(head[:, 3:4], redge[:, 1:2], redge[:, 3:4], ALU.is_equal))
            done(v.scalar_tensor_tensor(head[:, 3:4], head[:, 0:1], float(EPP), head[:, 3:4], ALU.is_equal, ALU.mult))
            done(v.scalar_tensor_tensor(head[:, 4:5], head[:, 3:4], 0.0, head[:, 2:3], ALU.is_equal, ALU.mult))
            done(v.tensor_scalar(head[:, 5:6], head[:, 4:5], -float(2 ** 21), float(2 ** 21), ALU.mult, ALU.add))
            done(v.tensor_tensor(head[:, 5:6], head[:, 5:6], head[:, 1:2], ALU.add))
            done(v.tensor_copy(head_idx[:, 0:1], head[:, 1:2]))
            done(v.tensor_copy(head_idx[:, 1:2], head[:, 5:6]))
            done(v.tensor_scalar(contrib[:], free128[:], part[:, 0:1], None, ALU.is_lt))
            done(v.scalar_tensor_tensor(contrib[:], rlast[:], redge[:, 0:1], contrib[:], ALU.is_equal, ALU.mult))
            def select_onehots(u, tiles, ready):
                for g in range(NG):
                    last = v.tensor_scalar(sel_onehot[:, g, tiles], code_sb[u][:, tiles], part_group[:, g:g + 1],
                                           None, ALU.is_equal)
                last.then_inc(ready, 1)

            def select_first(i, u):
                c = i * U + u
                dve.wait_ge(code_in[u], (i + 1) * 16)
                if not isinstance(c, int) or c:
                    dve.wait_ge(sel_mm, count(selected(i, u) - TS[u - 1] + 1))
                select_onehots(u, slice(0, P), sel_first_ready)

            def select_others(i, u):
                c = i * U + u
                dve.wait_ge(sel_mm, count(selected(i, u)))
                select_onehots(u, slice(P, TS[u] * P), sel_onehot_ready)
                return step(v.tensor_tensor(sel_mask[:], sel_node[:, ds(c * TSM, TSM)].unsqueeze(2).broadcast_to(
                    [P, TSM, GN]), free98[:, 0:GN].unsqueeze(1).broadcast_to([P, TSM, GN]), ALU.is_equal))

            def take_product(i, u, j):
                dve.wait_ge(sel_mm, count(selected(i, u) + j + 1))
                v.tensor_tensor(sel_prod, ps_sel[:, j % 2, 0:VW * GN].rearrange("p (f n) -> p f n", n=GN),
                                sel_mask[:, j:j + 1, :].broadcast_to([P, VW, GN]), ALU.mult).then_inc(sel_read, 1)

            def take_sum(i, u, j):
                dve.wait_ge(sel_read, count(selected(i, u) + j + 1))
                return step(v.tensor_reduce(gath[u][:, T - 1 - j, 0:VW], sel_prod, AX.X, ALU.add))

            def picks(c, u, g):
                dve.wait_ge(pick_mm, count(c * TG + g + 1))
                for j in range(G):
                    t = g * G + j
                    v.scalar_tensor_tensor(pick[:, t, :], free98[:], loc[u][:, t:t + 1],
                                           ps_pick[:, g % 2, j * NPP:(j + 1) * NPP], ALU.is_equal, ALU.mult,
                                           accum_out=dscore[:, t:t + 1]).then_inc(picked, 1)

            def sum_signs(c):
                dve.wait_ge(signs_mm, count(c))
                dve.wait_ge(signs_summed, count(c))
                v.tensor_tensor(sign_sums[:], sign_sums[:], ps_signs, ALU.add).then_inc(signs_summed, 1)

            def dst_onehot(i, u):
                dve.wait_ge(hib_in[u], (i + 1) * 16)
                v.tensor_scalar(onehot[:], hib_sb[u][:], part[:, 0:1], None, ALU.is_equal).then_inc(
                    onehot_ready, 1)

            def chunk(i, u, at, final):
                c = i * U + u
                after = (i if u < U - 1 else i + 1, (u + 1) % U)
                m = meta_sb[u]
                step(v.tensor_tensor(pen[:], dstc[u][:, 1:T + 1], dstc[u][:, 0:T], ALU.is_equal))
                k_type = step(v.tensor_copy(etc[:], m[:, 2 * T + 1:3 * T + 1]))
                dve.wait_ge(places_ready, c + 1)
                picks(c, u, 0)
                need(k_type, at)
                v.tensor_scalar(pen[:], pen[:], BIG, BIG, ALU.mult, ALU.subtract)
                k_mask = step(v.tensor_tensor(emask[:], etc[:].unsqueeze(2).broadcast_to([P, T, N_EDGE_TYPES]),
                                              types8[:].unsqueeze(1).broadcast_to([P, T, N_EDGE_TYPES]),
                                              ALU.is_equal))
                picks(c, u, 1)
                sum_signs(c)
                dve.wait_ge(eae_scaled, c + 1)
                dve.wait_ge(msg_mm, count(c))
                v.tensor_tensor(eae, eae_s, ps_attr[0:G * F_EDGE, :, 0:TG * P // 2], ALU.max).then_inc(
                    eae_ready, 1)
                need(k_mask, at)
                k_types = step(v.tensor_tensor(emask[:], emask[:], type_score[:].unsqueeze(1).broadcast_to(
                    [P, T, N_EDGE_TYPES]), ALU.mult))
                if not final:
                    k_sel = select_others(*after)
                need(k_types, at)
                k_types = step(v.tensor_reduce(escore[:], emask[:], AX.X, ALU.add))
                if not final:
                    need(k_sel, at)
                    take_product(*after, 0)
                picks(c, u, 2)
                if not final:
                    take_sum(*after, 0)
                    if not isinstance(i, int) or c + 2 < CHUNKS:
                        select_first(i if u < U - 2 else i + 1, (u + 2) % U)
                picks(c, u, 3)
                picks(c, u, 4)
                if not final:
                    dst_onehot(*after)
                dve.wait_ge(picked, count((c + 1) * T))
                need(k_types, at)
                k_score = step(v.tensor_tensor(escore[:], escore[:], dscore[:], ALU.add))
                dve.wait_ge(gathered[u], (i + 1) * (16 * (T - TS[u])))
                dve.wait_ge(msg_mm, count(c + 1))
                v.tensor_tensor(msg[:, 0:3 * G, :], gath[u][:, 0:3 * G, 0:VW],
                                ps_msg[:, 0, 0:3 * G * VW].rearrange("p (t f) -> p t f", f=VW), ALU.add)
                v.tensor_tensor(msg[:, 3 * G:T, :], gath[u][:, 3 * G:T, 0:VW],
                                ps_msg[:, 1, 0:2 * G * VW].rearrange("p (t f) -> p t f", f=VW),
                                ALU.add).then_inc(msg_added, 1)
                step(v.tensor_copy(mrun[:, 0:1], mrun[:, T:T + 1]))
                dve.wait_ge(msg_added, count(c + 1))
                need(k_score, at)
                k = step(v.tensor_tensor(alpha[:], msg[:, :, F_IN], escore[:], ALU.add))
                if not final:
                    take_product(*after, 1)
                need(k, at)
                k = step(v.scalar_tensor_tensor(alpha[:], alpha[:], SLOPE, alpha[:], ALU.mult, ALU.max))
                if not final:
                    take_sum(*after, 1)
                need(k, at)
                k = step(v.tensor_tensor_scan(mrun[:, 1:T + 1], pen[:], alpha[:], mrun[:, 0:1], ALU.add, ALU.max))
                if not final:
                    place(0, *after, at)
                need(k, at)
                k = step(v.tensor_tensor(args[:, 1, :], mrun[:, 0:T], pen[:], ALU.add))
                v.tensor_tensor(args[:, 0, :], alpha[:], mrun[:, 1:T + 1], ALU.subtract)
                need(k, at)
                v.tensor_tensor(args[:, 1, :], args[:, 1, :], mrun[:, 1:T + 1], ALU.subtract).then_inc(
                    args_ready, 1)
                if not final:
                    place(1, *after, at)
                dve.wait_ge(sums_ready, count(c))
                v.tensor_copy(terms[:, :, 0:1], sums[:, :, T:T + 1])
                if not final:
                    place(2, *after, at)
                if not final:
                    take_product(*after, 2)
                if not final:
                    place(3, *after, at)
                dve.wait_ge(exp_done, c + 1)
                v.tensor_copy(terms[:, F_IN, 1:T + 1], wts[:, 0, :])
                k = step(v.tensor_tensor(terms[:, 0:F_IN, 1:T + 1].rearrange("p f t -> p t f"), msg[:, :, 0:F_IN],
                                         wts[:, 0, :].unsqueeze(2).broadcast_to([P, T, F_IN]), ALU.mult))
                if not final:
                    k_take = take_sum(*after, 2)
                dve.wait_ge(keep_ready, c + 1)
                dve.wait_ge(rows_sums, count(c))
                need(k, at)
                v.tensor_tensor_scan(sums[:].rearrange("p f t -> p (f t)"), keep[:].rearrange("p f t -> p (f t)"),
                                     terms.rearrange("p f t -> p (f t)"), 0.0, ALU.mult,
                                     ALU.add).then_inc(sums_ready, 1)
                if not final:
                    for j in range(3, TS[after[1]]):
                        need(k_take, at)
                        take_product(*after, j)
                        k_take = take_sum(*after, j)

            dve.wait_ge(table_out, 16)
            select_first(0, 0)
            need(select_others(0, 0), 0)
            dst_onehot(0, 0)
            for j in range(TS[0]):
                take_product(0, 0, j)
                need(take_sum(0, 0, j), 0)
            select_first(0, 1)
            before = steps[0]
            STEPS = U * 16 + TS_ITER
            with dve.Fori(0, ITERS - 1) as i:
                for u in range(U):
                    chunk(i, u, i * STEPS, False)
            assert steps[0] == before + STEPS
            steps[0] = before + STEPS * (ITERS - 1)
            for u in range(U):
                chunk(ITERS - 1, u, 0, u == U - 1)

            sum_signs(CHUNKS)
            dve.wait_ge(signs_summed, count(CHUNKS + 1))
            done(v.tensor_copy(sign_parts[:, 0, :], sign_sums[:]))
            done(v.tensor_tensor(cnt[:], sign_sums[:], sign_parts[:, 0, :], ALU.subtract))
            done(v.tensor_copy(sign_parts[:, 1, :], cnt[:]))
            done(v.tensor_tensor(cnt[:], cnt[:], sign_parts[:, 1, :], ALU.subtract))
            v.tensor_copy(sign_parts[:, 2, :], cnt[:]).then_inc(sign_parts_ready, 1)
            dve.wait_ge(differ_mm, 1)
            done(v.tensor_scalar(fix[:, 0:1], ps_misc[:, 1, NPP - 1:NPP], -0.25, N_EDGES / 2 - 1.0, ALU.mult,
                                 ALU.add))
            done(v.scalar_tensor_tensor(fix[:, 0:1], sign_sums[:, NPP - 1:NPP], 0.5, fix[:, 0:1], ALU.mult, ALU.add))
            done(v.tensor_scalar(cnt[:], ps_misc[:, 1, 0:NPP], 0.25, fix[:, 0:1], ALU.mult, ALU.add))
            done(v.tensor_scalar(cnt[:], cnt[:], 0.0, None, ALU.max))
            done(v.tensor_scalar(scale[:, 0, :], node_id[:, 0:NPP], float(N_EDGES), None, ALU.add))
            done(v.tensor_tensor(scale[:, 0, :], scale[:, 0, :], cnt[:], ALU.subtract))
            done(v.scalar_tensor_tensor(cnt[:], scale[:, 0, :], unsorted[:, 0:1], cnt[:], ALU.mult, ALU.add))
            v.tensor_copy(pos[:], cnt[:]).then_inc(pos_ready, 1)

            flag = is_unsorted(dve)
            with dve.If(flag < 1):
                joined_step = stage(join_step)
                dve.wait_ge(tails_in, 16)
                v.tensor_copy(mtail[:], tails[:, VW:VW + 1].broadcast_to([P, P])).then_inc(head_idx_ready, 1)
                dve.wait_ge(mtail_mm, 1)
                joined_step(v.tensor_tensor(mtail[:], ps_misc[:, 0, 0:P], contrib[:], ALU.mult))
                joined_step(v.tensor_scalar(wtailT[:], contrib[:], BIG, BIG, ALU.mult, ALU.subtract))
                joined_step(v.tensor_tensor(mtail[:], mtail[:], wtailT[:], ALU.add))
                joined_step(v.tensor_reduce(fix[:, 0:1], mtail[:], AX.X, ALU.max))
                dve.wait_ge(own_in, 16)
                joined_step(v.tensor_tensor(fix[:, 0:1], fix[:, 0:1], own[:, VW:VW + 1], ALU.max))
                joined_step(v.tensor_tensor(fix[:, 1:2], own[:, VW:VW + 1], fix[:, 0:1], ALU.subtract))
                v.tensor_scalar(mtail[:], mtail[:], fix[:, 0:1], None, ALU.subtract).then_inc(targs_ready, 1)
                dve.wait_ge(wtailT_mm, 1)
                v.tensor_copy(wtailT[:], ps_misc[:, 0, P:2 * P]).then_inc(wtailT_sb, 1)
                v.tensor_copy(joined[:, VW:VW + 1], fix[:, 0:1])
                v.tensor_copy(joined[:, VW + 1:RW], own[:, VW + 1:RW])
                dve.wait_ge(tsum_mm, 1)
                v.scalar_tensor_tensor(joined[:, 0:VW], own[:, 0:VW], fix[:, 2:3], ps_misc[:, 0, 2 * P:2 * P + VW],
                                       ALU.mult, ALU.add).then_inc(joined_ready, 1)
            with dve.If(flag >= 1):
                merged_step = stage(merge_step)
                merged_step(v.tensor_scalar(before_me[:], free128[:], part[:, 0:1], None, ALU.is_gt))
                merged_step(v.memset(mg[:], 0.0))
                STEPS = 14
                with dve.Fori(0, EPP) as t:
                    at = t * STEPS
                    dve.wait_ge(tile_in, t * 32 + 32)
                    merged_step(v.tensor_scalar(mg[:, 0:1], mg[:, 0:1], 1.0, None, ALU.add), at)
                    merged_step(v.tensor_scalar(mg[:, 1:2], mg[:, 0:1], float(EPP), None, ALU.is_equal), at)
                    merged_step(v.tensor_tensor(mg[:, 2:3], tile_rows[:, VW + 1:RW], next_row[:, 1:2], ALU.not_equal), at)
                    merged_step(v.tensor_tensor(mg[:, 1:2], mg[:, 1:2], mg[:, 2:3], ALU.max), at)
                    merged_step(v.tensor_scalar(mg[:, 3:4], tile_rows[:, VW + 1:RW], part[:, 0:1], 1.0, ALU.add,
                                                ALU.add), at)
                    merged_step(v.scalar_tensor_tensor(mg[:, 3:4], mg[:, 3:4], mg[:, 1:2], part[:], ALU.mult,
                                                       ALU.subtract), at)
                    merged_step(v.tensor_scalar(mg[:, 3:4], mg[:, 3:4], -1.0, None, ALU.add), at)
                    v.tensor_copy(mtail[:], mg[:, 3:4].broadcast_to([P, P]))
                    v.tensor_copy(contrib[:], tile_rows[:, VW:VW + 1].broadcast_to([P, P])).then_inc(merge_keys, 1)
                    v.tensor_scalar(merge_idx[:, 0:1], tile_rows[:, VW + 1:RW], float(N_EDGES), None,
                                    ALU.add).then_inc(merge_idx_ready, 1)
                    dve.wait_ge(merge_keys_mm, t + 1)
                    merged_step(v.tensor_scalar(wtailT[:], ps_misc[:, 0, 0:P], mg[:, 3:4], None, ALU.is_equal), at)
                    merged_step(v.tensor_tensor(mtail[:], wtailT[:], ps_misc[:, 0, P:2 * P], ALU.mult), at)
                    v.tensor_tensor(contrib[:], wtailT[:], before_me[:], ALU.mult)
                    merged_step(v.tensor_scalar(wtailT[:], wtailT[:], BIG, BIG, ALU.mult, ALU.subtract), at)
                    v.tensor_tensor(mtail[:], mtail[:], wtailT[:], ALU.add)
                    merged_step(v.tensor_reduce(mg[:, 5:6], contrib[:], AX.X, ALU.add), at)
                    v.scalar_tensor_tensor(mg[:, 5:6], mg[:, 5:6], 0.0, mg[:, 1:2], ALU.is_equal, ALU.mult)
                    merged_step(v.tensor_reduce(fix[:, 0:1], mtail[:], AX.X, ALU.max), at)
                    merged_step(v.tensor_scalar(mg[:, 5:6], mg[:, 5:6], -float(2 ** 21), float(2 ** 21) + N_EDGES,
                                                ALU.mult, ALU.add), at)
                    dve.wait_ge(node_in, t * 16 + 16)
                    v.tensor_tensor(merge_idx[:, 1:2], mg[:, 5:6], tile_rows[:, VW + 1:RW], ALU.add)
                    merged_step(v.tensor_tensor(fix[:, 0:1], fix[:, 0:1], own[:, VW:VW + 1], ALU.max), at)
                    v.tensor_tensor(fix[:, 1:2], own[:, VW:VW + 1], fix[:, 0:1], ALU.subtract)
                    v.tensor_scalar(mtail[:], mtail[:], fix[:, 0:1], None, ALU.subtract).then_inc(merge_args, 1)
                    dve.wait_ge(merge_wT_mm, t + 1)
                    v.tensor_copy(wtailT[:], ps_misc[:, 1, 0:P]).then_inc(merge_wT_sb, 1)
                    v.tensor_copy(joined[:, VW:VW + 1], fix[:, 0:1])
                    v.tensor_copy(joined[:, VW + 1:RW], tile_rows[:, VW + 1:RW])
                    dve.wait_ge(merge_sum_mm, t + 1)
                    v.scalar_tensor_tensor(joined[:, 0:VW], own[:, 0:VW], fix[:, 2:3],
                                           ps_misc[:, 1, 2 * P:2 * P + VW], ALU.mult,
                                           ALU.add).then_inc(merge_row_ready, 1)
            finished = stage(last_step)
            dve.wait_ge(x_in, 48)
            for k, n in enumerate((slice(0, PIECE), slice(PIECE, NPP))):
                w = n.stop - n.start
                dve.wait_ge(last_in[k], 16 * w)
                finished(v.tensor_tensor(scale[:, 0, n], last_rows[:, n, VW + 1], node_id[:, n], ALU.is_equal))
                finished(v.tensor_scalar(scale[:, 1, n], last_rows[:, n, F_IN], 1e-16, None, ALU.add))
                finished(v.reciprocal(scale[:, 1, n], scale[:, 1, n]))
                finished(v.tensor_tensor(scale[:, 0, n], scale[:, 0, n], scale[:, 1, n], ALU.mult))
                finished(v.tensor_tensor(h[:, n, :], last_rows[:, n, 0:F_IN],
                                         scale[:, 0, n].unsqueeze(2).broadcast_to([P, w, F_IN]), ALU.mult))
                v.tensor_tensor(h[:, n, :], h[:, n, :], x_sb[:, n, :], ALU.add).then_inc(out_ready, 1)


def kernel(x, src, dst, edge_attr_16, edge_type_8, node_type_4, L0_gnn_hetero_w, L0_gnn_hetero_b,
           L0_gnn_edge_type_emb, L0_gnn_edge_attr_w, L0_gnn_att_w, L0_gnn_lin_w):
    import numpy as np
    import concourse.bacc as bacc
    from concourse.bass_utils import run_bass_kernel_spmd

    x, src, dst = np.asarray(x), np.asarray(src), np.asarray(dst)
    node_type, edge_type = np.asarray(node_type_4), np.asarray(edge_type_8)
    pad = N_PAD - N_NODES
    rows = dst.reshape(P, EPP)
    before = np.full((P, 1), -1, dst.dtype)
    dst_prev = np.concatenate([before, rows], axis=1)
    windows = np.stack([dst_prev[:, c * T:(c + 1) * T + 1] for c in range(CHUNKS)], axis=1)
    meta = np.concatenate([src.reshape(P, CHUNKS, T), windows, edge_type.reshape(P, CHUNKS, T)], axis=2)
    none = np.full((1,), -1, dst.dtype)
    row_edges = np.stack([rows[:, 0], rows[:, -1], np.concatenate([none, rows[:-1, -1]]),
                          np.concatenate([rows[1:, 0], none])], axis=1)
    attr = np.asarray(edge_attr_16).reshape(P, CHUNKS, TG, G, F_EDGE).transpose(3, 4, 1, 2, 0)
    sel = src.reshape(P, CHUNKS, T)[:, :, :T - 1 - TSM:-1]
    arrays = {
        "x_in": np.concatenate([x, np.zeros((pad, F_IN), x.dtype)]).reshape(P, NPP, F_IN),
        "meta_in": meta,
        "dst_rows_in": rows,
        "dst_tmajor_in": rows.T.reshape(P, EPP),
        "sel_src_in": np.concatenate([sel.transpose(1, 2, 0).reshape(P, SEL), sel.reshape(P, SEL)], axis=1),
        "row_edges_in": row_edges,
        "row_last_in": rows[:, -1],
        "edge_attr_t_in": attr.reshape(G * F_EDGE, CHUNKS, TG * P),
        "node_type_in": np.concatenate([node_type, np.zeros((pad,), node_type.dtype)]).reshape(P, NPP),
        "hetero_wT_in": np.asarray(L0_gnn_hetero_w).transpose(2, 0, 1).reshape(F_IN, N_NODE_TYPES * F_IN),
        "hetero_bT_in": np.asarray(L0_gnn_hetero_b).T,
        "edge_type_emb_in": np.asarray(L0_gnn_edge_type_emb),
        "edge_attr_w_in": np.asarray(L0_gnn_edge_attr_w),
        "att_w_in": np.asarray(L0_gnn_att_w),
        "lin_w_in": np.asarray(L0_gnn_lin_w),
    }
    nc = bacc.Bacc("TRN2", target_bir_lowering=False, num_devices=1)
    args = []
    for name in list(arrays):
        arrays[name] = np.ascontiguousarray(arrays[name])
        args.append(nc.dram_tensor(name, arrays[name].shape, mybir.dt.from_np(arrays[name].dtype),
                                   kind="ExternalInput").ap())
    out = nc.dram_tensor("out_dram", (P, NPP, F_IN), mybir.dt.float32, kind="ExternalOutput").ap()
    gnn_kernel(nc, *args, out)
    result = run_bass_kernel_spmd(nc, [arrays], core_ids=[0])
    return result.results[0]["out_dram"].reshape(N_PAD, F_IN)[:N_NODES]
```
